# Optimizing a Trainium2 kernel written in Bass

```python
import numpy as np
import jax
import jax.numpy as jnp

def _softmax(x, axis=-1):
    return jax.nn.softmax(x, axis=axis)

def _gelu(x):
    return jax.nn.gelu(x, approximate=True)

def _silu(x):
    return jax.nn.silu(x)

def _sigmoid(x):
    return jax.nn.sigmoid(x)

def _layernorm(x, axis=-1, eps=1e-05):
    m = jnp.mean(x, axis=axis, keepdims=True)
    v = jnp.var(x, axis=axis, keepdims=True)
    return (x - m) / jnp.sqrt(v + eps)

def _scatter_add(tgt, idx, src, axis=0):
    return tgt.at[idx].add(src)

def _segment_sum(src, seg, n):
    return jax.ops.segment_sum(src, seg, n)
kernel_name = 'mk_vit_tower_d1_tok_img256_r4_dc8b57'

def setup_inputs(seed: int=0):
    np.random.seed(seed)
    _w = jnp.asarray

    def _rec_inputs():
        import jax
        import jax.numpy as jnp
        _rk = jax.random.key(seed)
        x = -0.000928989 + 1.00043 * jax.random.normal(jax.random.fold_in(_rk, 1), (128, 64, 64, 1), jnp.float32)
        return x
    x = _rec_inputs()

    def _L0_tok_setup():
        import jax, jax.numpy as jnp
        import numpy as np
        L = 4
        M1 = 12
        M2 = 12
        BN_EPS = 1e-05

        def _fourier_layer(v, W1, W2):
            B, C, Sx, Sy = v.shape
            x_ft = jnp.fft.rfft2(v)
            out1 = jnp.einsum('bixy,ioxy->boxy', x_ft[:, :, :M1, :M2], W1)
            out2 = jnp.einsum('bixy,ioxy->boxy', x_ft[:, :, -M1:, :M2], W2)
            out_ft = jnp.zeros((B, C, Sx, Sy // 2 + 1), jnp.complex64)
            out_ft = out_ft.at[:, :, :M1, :M2].set(out1)
            out_ft = out_ft.at[:, :, Sx - M1:, :M2].set(out2)
            return jnp.fft.irfft2(out_ft, s=(Sx, Sy))
        key = jax.random.key(seed)
        ks = jax.random.split(key, 10)
        B, S, d_a, d_v, d_u = (16, 64, 3, 32, 1)
        return {'x': jax.random.normal(ks[0], (B, S, S, 1), jnp.float32), 'p_w': jax.random.normal(ks[1], (d_a, d_v), jnp.float32) * 0.3, 'p_b': jax.random.normal(ks[2], (d_v,), jnp.float32) * 0.1, 'fw1': jax.random.normal(ks[3], (L, d_v, d_v, M1, M2, 2), jnp.float32) * (1.0 / d_v), 'fw2': jax.random.normal(ks[4], (L, d_v, d_v, M1, M2, 2), jnp.float32) * (1.0 / d_v), 'w_w': jax.random.normal(ks[5], (L, d_v, d_v), jnp.float32) * (1.0 / np.sqrt(d_v)), 'w_b': jax.random.normal(ks[6], (L, d_v), jnp.float32) * 0.1, 'bn_g': jnp.ones((L, d_v), jnp.float32), 'bn_b': jnp.zeros((L, d_v), jnp.float32), 'q_w': jax.random.normal(ks[7], (d_v, d_u), jnp.float32) * 0.3, 'q_b': jax.random.normal(ks[8], (d_u,), jnp.float32) * 0.1}
    _L0_tok_all = _L0_tok_setup()
    _L0_tok_in = {k: v for k, v in _L0_tok_all.items() if k in ('p_w', 'p_b', 'fw1', 'fw2', 'w_w', 'w_b', 'bn_g', 'bn_b', 'q_w', 'q_b')}
    del _L0_tok_all

    def _L0_attn_setup():
        import jax, jax.numpy as jnp
        import numpy as np
        WS = 7
        CT = 2
        H = 8
        C = 64
        B = 1024
        WS2 = WS * WS
        N = WS2 + CT * CT
        HD = C // H

        def _relative_position_index():
            coords = np.arange(WS)
            cc = np.stack(np.meshgrid(coords, coords, indexing='ij'))
            cc = cc.reshape(2, -1)
            rel = cc[:, :, None] - cc[:, None, :]
            rel = rel.transpose(1, 2, 0).copy()
            rel[:, :, 0] += WS - 1
            rel[:, :, 1] += WS - 1
            rel[:, :, 0] *= 2 * WS - 1
            return jnp.asarray(rel.sum(-1).reshape(-1), dtype=jnp.int32)
        key = jax.random.key(seed)
        k1, k2, k3, k4, k5 = jax.random.split(key, 5)
        s = 0.02
        return {'x': jax.random.normal(k1, (B, N, C), dtype=jnp.float32), 'w_qkv': jax.random.normal(k2, (3 * C, C), dtype=jnp.float32) * s, 'w_proj': jax.random.normal(k3, (C, C), dtype=jnp.float32) * s, 'b_proj': jax.random.normal(k4, (C,), dtype=jnp.float32) * s, 'rel_table': jax.random.normal(k5, ((2 * WS - 1) ** 2, H), dtype=jnp.float32) * s, 'rel_index': _relative_position_index()}
    _L0_attn_all = _L0_attn_setup()
    _L0_attn_in = {k: v for k, v in _L0_attn_all.items() if k in ('w_qkv', 'w_proj', 'b_proj', 'rel_table', 'rel_index')}
    del _L0_attn_all

    def _L0_ffn_setup():
        import jax, jax.numpy as jnp
        import numpy as np
        B, S, H, F, E, K = (8, 1024, 64, 128, 16, 2)
        EPS = 1e-05
        key = jax.random.key(seed)
        ks = jax.random.split(key, 9)
        sc = 0.02
        return {'x': jax.random.normal(ks[0], (B, S, H), dtype=jnp.float32), 'gate_w': jax.random.normal(ks[1], (H, E), dtype=jnp.float32) * sc, 'gate_b': jnp.zeros((E,), dtype=jnp.float32), 'w1': jax.random.normal(ks[2], (E, H, F), dtype=jnp.float32) * sc, 'b1': jnp.zeros((E, F), dtype=jnp.float32), 'w2': jax.random.normal(ks[3], (E, F, H), dtype=jnp.float32) * sc, 'b2': jnp.zeros((E, H), dtype=jnp.float32), 'gamma': jnp.ones((H,), dtype=jnp.float32), 'beta': jnp.zeros((H,), dtype=jnp.float32)}
    _L0_ffn_all = _L0_ffn_setup()
    _L0_ffn_in = {k: v for k, v in _L0_ffn_all.items() if k in ('gate_w', 'gate_b', 'w1', 'b1', 'w2', 'b2', 'gamma', 'beta')}
    del _L0_ffn_all
    return {'x': x, 'L0_tok_p_w': _L0_tok_in['p_w'], 'L0_tok_p_b': _L0_tok_in['p_b'], 'L0_tok_fw1': _L0_tok_in['fw1'], 'L0_tok_fw2': _L0_tok_in['fw2'], 'L0_tok_w_w': _L0_tok_in['w_w'], 'L0_tok_w_b': _L0_tok_in['w_b'], 'L0_tok_bn_g': _L0_tok_in['bn_g'], 'L0_tok_bn_b': _L0_tok_in['bn_b'], 'L0_tok_q_w': _L0_tok_in['q_w'], 'L0_tok_q_b': _L0_tok_in['q_b'], 'L0_attn_w_qkv': _L0_attn_in['w_qkv'], 'L0_attn_w_proj': _L0_attn_in['w_proj'], 'L0_attn_b_proj': _L0_attn_in['b_proj'], 'L0_attn_rel_table': _L0_attn_in['rel_table'], 'L0_attn_rel_index': _L0_attn_in['rel_index'], 'L0_ffn_gate_w': _L0_ffn_in['gate_w'], 'L0_ffn_gate_b': _L0_ffn_in['gate_b'], 'L0_ffn_w1': _L0_ffn_in['w1'], 'L0_ffn_b1': _L0_ffn_in['b1'], 'L0_ffn_w2': _L0_ffn_in['w2'], 'L0_ffn_b2': _L0_ffn_in['b2'], 'L0_ffn_gamma': _L0_ffn_in['gamma'], 'L0_ffn_beta': _L0_ffn_in['beta']}

def reference(x, L0_tok_p_w, L0_tok_p_b, L0_tok_fw1, L0_tok_fw2, L0_tok_w_w, L0_tok_w_b, L0_tok_bn_g, L0_tok_bn_b, L0_tok_q_w, L0_tok_q_b, L0_attn_w_qkv, L0_attn_w_proj, L0_attn_b_proj, L0_attn_rel_table, L0_attn_rel_index, L0_ffn_gate_w, L0_ffn_gate_b, L0_ffn_w1, L0_ffn_b1, L0_ffn_w2, L0_ffn_b2, L0_ffn_gamma, L0_ffn_beta):
    import jax
    import jax.numpy as jnp

    def _L0_tok_ref(x, p_w, p_b, fw1, fw2, w_w, w_b, bn_g, bn_b, q_w, q_b):
        import jax, jax.numpy as jnp
        import numpy as np
        L = 4
        M1 = 12
        M2 = 12
        BN_EPS = 1e-05

        def _fourier_layer(v, W1, W2):
            B, C, Sx, Sy = v.shape
            x_ft = jnp.fft.rfft2(v)
            out1 = jnp.einsum('bixy,ioxy->boxy', x_ft[:, :, :M1, :M2], W1)
            out2 = jnp.einsum('bixy,ioxy->boxy', x_ft[:, :, -M1:, :M2], W2)
            out_ft = jnp.zeros((B, C, Sx, Sy // 2 + 1), jnp.complex64)
            out_ft = out_ft.at[:, :, :M1, :M2].set(out1)
            out_ft = out_ft.at[:, :, Sx - M1:, :M2].set(out2)
            return jnp.fft.irfft2(out_ft, s=(Sx, Sy))
        B, Sx, Sy, _ = x.shape
        gx = jnp.broadcast_to(jnp.linspace(0.0, 1.0, Sx, dtype=jnp.float32)[None, :, None, None], (B, Sx, Sy, 1))
        gy = jnp.broadcast_to(jnp.linspace(0.0, 1.0, Sy, dtype=jnp.float32)[None, None, :, None], (B, Sx, Sy, 1))
        h = jnp.concatenate([x, gx, gy], axis=-1)
        v = h @ p_w + p_b
        v = jnp.transpose(v, (0, 3, 1, 2))
        for i in range(L):
            W1 = fw1[i, ..., 0] + 1j * fw1[i, ..., 1]
            W2 = fw2[i, ..., 0] + 1j * fw2[i, ..., 1]
            x1 = _fourier_layer(v, W1, W2)
            x2 = jnp.einsum('bcxy,cd->bdxy', v, w_w[i]) + w_b[i][None, :, None, None]
            v = x1 + x2
            mean = jnp.mean(v, axis=(0, 2, 3), keepdims=True)
            var = jnp.var(v, axis=(0, 2, 3), keepdims=True)
            v = (v - mean) * jax.lax.rsqrt(var + BN_EPS)
            v = v * bn_g[i][None, :, None, None] + bn_b[i][None, :, None, None]
            if i < L - 1:
                v = jax.nn.relu(v)
        out = jnp.einsum('bcxy,cu->bxyu', v, q_w) + q_b
        return jnp.squeeze(out)

    def _L0_attn_ref(x, w_qkv, w_proj, b_proj, rel_table, rel_index):
        import jax, jax.numpy as jnp
        import numpy as np
        WS = 7
        CT = 2
        H = 8
        C = 64
        B = 1024
        WS2 = WS * WS
        N = WS2 + CT * CT
        HD = C // H

        def _relative_position_index():
            coords = np.arange(WS)
            cc = np.stack(np.meshgrid(coords, coords, indexing='ij'))
            cc = cc.reshape(2, -1)
            rel = cc[:, :, None] - cc[:, None, :]
            rel = rel.transpose(1, 2, 0).copy()
            rel[:, :, 0] += WS - 1
            rel[:, :, 1] += WS - 1
            rel[:, :, 0] *= 2 * WS - 1
            return jnp.asarray(rel.sum(-1).reshape(-1), dtype=jnp.int32)
        b, n, c = x.shape
        scale = HD ** (-0.5)
        qkv = jnp.einsum('bnc,dc->bnd', x, w_qkv).reshape(b, n, 3, H, HD)
        qkv = jnp.moveaxis(qkv, 2, 0)
        q, k, v = (qkv[0], qkv[1], qkv[2])
        attn = jnp.einsum('bnhd,bmhd->bhnm', q, k) * scale
        bias = rel_table[rel_index].reshape(WS2, WS2, H).transpose(2, 0, 1)
        pad = n - WS2
        bias = jnp.pad(bias, ((0, 0), (pad, 0), (pad, 0)))
        attn = jax.nn.softmax(attn + bias[None], axis=-1)
        out = jnp.einsum('bhnm,bmhd->bnhd', attn, v).reshape(b, n, c)
        return jnp.einsum('bnc,dc->bnd', out, w_proj) + b_proj

    def _L0_ffn_ref(x, gate_w, gate_b, w1, b1, w2, b2, gamma, beta):
        import jax, jax.numpy as jnp
        import numpy as np
        B, S, H, F, E, K = (8, 1024, 64, 128, 16, 2)
        EPS = 1e-05
        gate_logits = x @ gate_w + gate_b
        topk_vals, topk_idx = jax.lax.top_k(gate_logits, K)
        topk_w = jax.nn.softmax(topk_vals, axis=-1)
        h = jax.nn.relu(jnp.einsum('bsh,ehf->bsef', x, w1) + b1)
        expert_out = jnp.einsum('bsef,efh->bseh', h, w2) + b2
        sel = jnp.take_along_axis(expert_out, topk_idx[:, :, :, None], axis=2)
        moe = jnp.sum(topk_w[..., None] * sel, axis=2)
        y = x + moe
        mu = jnp.mean(y, axis=-1, keepdims=True)
        var = jnp.var(y, axis=-1, keepdims=True)
        return (y - mu) / jnp.sqrt(var + EPS) * gamma + beta
    h = _L0_tok_ref(x, L0_tok_p_w, L0_tok_p_b, L0_tok_fw1, L0_tok_fw2, L0_tok_w_w, L0_tok_w_b, L0_tok_bn_g, L0_tok_bn_b, L0_tok_q_w, L0_tok_q_b)
    h = h + _L0_attn_ref(_layernorm(h, axis=-1), L0_attn_w_qkv, L0_attn_w_proj, L0_attn_b_proj, L0_attn_rel_table, L0_attn_rel_index)
    h = h + _L0_ffn_ref(_layernorm(h, axis=-1), L0_ffn_gate_w, L0_ffn_gate_b, L0_ffn_w1, L0_ffn_b1, L0_ffn_w2, L0_ffn_b2, L0_ffn_gamma, L0_ffn_beta)
    return h

_drawn_inputs = setup_inputs


def setup_inputs(seed=0):
    import zlib

    import numpy as np

    out = dict(_drawn_inputs(seed))
    spreads = {'L0_tok_bn_g': (1.0, 0.2),
     'L0_tok_bn_b': (0.0, 0.1),
     'L0_ffn_gate_b': (0.0, 0.285),
     'L0_ffn_b1': (0.0, 0.8),
     'L0_ffn_b2': (0.0, 0.291),
     'L0_ffn_gamma': (1.0, 0.2),
     'L0_ffn_beta': (0.0, 0.1)}
    factors = {'L0_tok_p_b': 8.0,
     'L0_tok_w_b': 8.0,
     'L0_attn_w_qkv': 7.663,
     'L0_attn_w_proj': 7.778,
     'L0_attn_b_proj': 3.311,
     'L0_attn_rel_table': 8.0,
     'L0_ffn_w1': 8.0,
     'L0_ffn_w2': 6.668}
    for name, (base, spread) in spreads.items():
        noise = np.random.default_rng([zlib.crc32(name.encode()), seed]).standard_normal(out[name].shape)
        drawn = base * np.exp(spread * noise) if base else spread * noise
        out[name] = jnp.asarray(drawn.astype(out[name].dtype))
    for name, factor in factors.items():
        out[name] = (out[name] * factor).astype(out[name].dtype)
    return out
```

```python
from contextlib import ExitStack

import numpy as np

import concourse.bass as bass
from concourse import mybir

F32 = mybir.dt.float32
F16 = mybir.dt.float16
I32 = mybir.dt.int32
U32 = mybir.dt.uint32
ALU = mybir.AluOpType
ACT = mybir.ActivationFunctionType
AX = mybir.AxisListType

B, S, C, L = 128, 64, 32, 4
PX = S * S
M1 = M2 = 12
KX, KYH, KY4 = 2 * M1, M2 // 4, 4
P = 128
GI = P // C
NG = B // GI
HG = NG // 2
MODES = KYH * KX
SPEC = MODES * 2
CH = 6
NCH = MODES // CH
MJ = CH // 2
MIX_BANKS = 2 * MJ
TJ, YJ, T2J, XJ = 8, 4, 3, 2
T3J, XIJ, T4J, FJ = 3, 3, 4, 8
F0B = 16
F0J = 6
NF0 = B // F0B
FQ = F0B * SPEC
EPS = 1e-5
BN_STEPS = 13


def pipelined(eng, step, fresh=False):
    step(0, 0, 0, True, False)
    if fresh:
        step(1, 0, 1, True, True)
        step(2, 1, 0, True, True)
    with eng.Fori(1 if fresh else 0, HG - 1) as i:
        step(i * 2 + 1, i, 1, True, True)
        step(i * 2 + 2, i + 1, 0, True, True)
    step(NG - 1, HG - 1, 1, True, True)
    step(NG, HG, 0, False, True)


def half_before(h, par):
    return h if par else h - 1


def by_pairs(eng, layer, count, step):
    if isinstance(layer, int):
        step(0, 0, 0)
        step(1, 0, 1)
    with eng.Fori(1 if isinstance(layer, int) else 0, count // 2) as i:
        step(i * 2, i, 0)
        step(i * 2 + 1, i, 1)


INVERSE = (("t3", 0), ("t3", 1), ("final", 0), ("t3", 2), ("final", 1), ("final", 2), ("xi", 0), ("xi", 1), ("final", 3),
           ("xi", 2), ("final", 4), ("t4", 0), ("t4", 1), ("final", 5), ("t4", 2), ("final", 6), ("t4", 3), ("final", 7))


def inverse_order(head, tail, **jobs):
    for name, i in INVERSE:
        if name in jobs and (tail if name == "final" else head):
            jobs[name](i)


def reuse(eng, done, per, n):
    if not isinstance(n, int):
        eng.wait_ge(done, (n - 1) * per)
    elif n >= 2:
        eng.wait_ge(done, (n - 1) * per)


def bank_free(eng, emptied, job, ring=2):
    if not isinstance(job, int) or job >= ring:
        eng.wait_ge(emptied, job - (ring - 1))


def forward_use(l):
    return l * (2 * NG) - NG


def inverse_use(l):
    return l * (2 * NG)


FINAL_USE = L * 2 * NG - NG


def build(nc, x, fw, wmix, chan, p16, pt7, grid, gspec, fwd_y, fwd_x, inv_x, inv_y, ident, ident16, avg, quarter,
          qbd, qb, att, moe, out):
    u_dram = nc.dram_tensor("u_pixels", [NG, P, PX], F32, kind="Internal").ap()
    fx_dram = nc.dram_tensor("x_spectrum", [B, KYH, KY4, 2 * KX], F32, kind="Internal").ap()
    h_dram = nc.dram_tensor("h_tokens", [NG, GI, PX], F32, kind="Internal").ap()

    with ExitStack() as ctx:
        def sem(name):
            return ctx.enter_context(nc.semaphore(name))

        def pair(name):
            return [sem(f"{name}{s}") for s in range(2)]

        bank = [ctx.enter_context(nc.psum_tensor(f"bank{i}", [P, 512], F32)) for i in range(8)]

        fno = ExitStack()

        def sb(name, shape, dt=F32):
            return fno.enter_context(nc.sbuf_tensor(name, shape, dt))

        spec = sb("spec", [P, B, SPEC])
        v = [sb(f"v{s}", [P, PX]) for s in range(2)]
        pix = [sb(f"pix{s}", [P, PX]) for s in range(2)]
        rowf = [sb(f"rowf{s}", [P, 2 * M2 * S]) for s in range(2)]
        rowt = [sb(f"rowt{s}", [P, 2 * M2 * S]) for s in range(2)]
        wide = sb("wide", [P, 2 * CH * 3 * P])
        og = [sb(f"og{s}", [P, GI * SPEC]) for s in range(2)]
        wd = [sb(f"wd{s}", [P, CH * 2 * C]) for s in range(2)]
        stats = sb("stats", [P, NG * FJ * 6])
        wm = sb("wm", [P, L, P])
        wcur = sb("wcur", [P, P])
        wx7 = sb("wx7", [7, P])
        pt7_sb = sb("pt7_sb", [P, 7])
        p16_sb = sb("p16_sb", [16, P])
        fy = sb("fy", [P, 2, 48], F16)
        fx = sb("fx", [P, 2, 48], F16)
        ix = sb("ix", [96, 2, P], F16)
        idn16 = sb("idn16", [P, P], F16)
        iy = sb("iy", [96, 256])
        idn = sb("idn", [P, P])
        avg_sb = sb("avg_sb", [P, P])
        quarter_sb = sb("quarter_sb", [P, P])
        chan_sb = sb("chan_sb", [P, L, 3])
        qbd_sb = sb("qbd_sb", [P, GI + 1])
        qcol = sb("qcol", [P, GI])
        qb_sb = sb("qb_sb", [P, 1])
        bn = sb("bn", [P, 32])
        fno.close()

        HALF = CH * 3 * P
        bd = [wide[:, s * HALF:(s + 1) * HALF].rearrange("p (m t n) -> p m t n", m=CH, t=3) for s in range(2)]
        ht = [wide[0:96, s * 2048:(s + 1) * 2048].rearrange("p (q n) -> p q n", q=16) for s in range(2)]
        f0_rows = [wide[0:16, s * FQ:(s + 1) * FQ] for s in range(2)]
        spec_flat = spec[:, :, :].rearrange("p b s -> p (b s)")

        def halves(t):
            n = t.shape[1] // 2
            return t[:, 0:n].bitcast(F16), t[:, n:2 * n].bitcast(F16)

        pix_hi, pix_lo = zip(*[halves(t) for t in pix])
        rowt_hi, rowt_lo = zip(*[halves(t) for t in rowt])
        og16 = [t[:, :].bitcast(F16).rearrange("p (n t m) -> p n t m", t=2, m=2 * KX) for t in og]
        kxt = [t[0:96, 0:M2 * P // 2].bitcast(F16) for t in rowt]
        wds = [t[:, :].rearrange("p (m r o) -> p m r o", m=CH, r=2) for t in wd]
        bias_l = bn[:, 16:17]
        scale_l = bn[:, 17:18]
        gamma, beta, wb = bn[:, 18:19], bn[:, 19:20], bn[:, 20:21]
        hconst = bn[:, 21:22]

        waited = sem("waited")
        const_in, x_in, f0_const_in, fx_out = sem("const_in"), sem("x_in"), sem("f0_const_in"), sem("fx_out")
        f0_in, v_in, x7_in, wd_in = pair("f0_in"), pair("v_in"), pair("x7_in"), pair("wd_in")
        v_used, relu_done = sem("v_used"), sem("relu_done")
        t_done, t_hi, t_out = sem("t_done"), sem("t_hi"), sem("t_out")
        y_done, y_out = sem("y_done"), sem("y_out")
        t2_done, t2_hi, t2_out = sem("t2_done"), sem("t2_hi"), sem("t2_out")
        x_done, x_out = sem("x_done"), sem("x_out")
        f0_done, f0_out = sem("f0_done"), pair("f0_out")
        bd_zero, bd_ready = sem("bd_zero"), sem("bd_ready")
        mix_done, mix_out = sem("mix_done"), sem("mix_out")
        og_hi, og_ready = sem("og_hi"), sem("og_ready")
        t3_done, t3_out = sem("t3_done"), sem("t3_out")
        xi_done, xi_out = sem("xi_done"), sem("xi_out")
        t4_done, t4_out = sem("t4_done"), sem("t4_out")
        fin_done, fin_out = sem("fin_done"), sem("fin_out")
        stats_done = sem("stats_done")
        u_stored = pair("u_stored")
        w_ready, w7_done, w7_ready = sem("w_ready"), sem("w7_done"), sem("w7_ready")
        bn_step, bn_avg, bn_sqrt = sem("bn_step"), sem("bn_avg"), sem("bn_sqrt")
        q_step, q_sum, q_ready = sem("q_step"), sem("q_sum"), sem("q_ready")
        head_done, head_out = sem("head_done"), pair("head_out")
        h_stored = pair("h_stored")

        consts = ((fy, fwd_y), (fx, fwd_x), (ix, inv_x), (iy, inv_y), (idn, ident), (idn16, ident16), (avg_sb, avg),
                  (quarter_sb, quarter), (wm, wmix), (chan_sb, chan), (p16_sb, p16), (pt7_sb, pt7),
                  (qbd_sb, qbd), (qb_sb, qb))
        CONST = 16 * len(consts)

        tok_sync, tok_gpsimd, tok_tensor, tok_scalar, tok_vector = token_programs(
            nc, ctx, bank, sem, h_dram, h_stored, att, moe, out)
        block = ctx.enter_context(nc.Block())

        def alone(eng):
            eng.sem_inc(waited, 1)

        @block.sync
        def _(sp):
            for dst, src in consts:
                sp.dma_start(dst[:], src).then_inc(const_in, 16)
            sp.dma_start(v[0][:, :], x.rearrange("g i n -> (g i) n")).then_inc(x_in, 16)
            for s in range(2):
                sp.dma_start(f0_rows[s][4:16, :], gspec).then_inc(f0_const_in, 16)
                sp.dma_start(wd[s][:, :], fw[s]).then_inc(wd_in[s], 16)
            sp.wait_ge(x_out, XJ)
            sp.dma_start(fx_dram.rearrange("b h k m -> b (h k m)"), og[0][:, :]).then_inc(fx_out, 16)
            sp.wait_ge(fx_out, 16)
            for q in range(NF0):
                if q >= 2:
                    sp.wait_ge(f0_done, F0J * (q - 1))
                for k4 in range(KY4):
                    sp.dma_start(f0_rows[q % 2][k4:k4 + 1, :].rearrange("k (b h m) -> k b h m", b=F0B, h=KYH),
                                 fx_dram[q * F0B:(q + 1) * F0B, :, k4:k4 + 1, :].rearrange("b h k m -> k b h m"))\
                      .then_inc(f0_in[q % 2], 16)

            def load_weights(first):
                with sp.Fori(1, NCH // 2) as i:
                    for par in range(2):
                        sp.wait_ge(bd_ready, first + i * 2 + par - 1)
                        sp.dma_start(wd[par][:, :], fw[first + i * 2 + par]).then_inc(wd_in[par], 16)

            def store(l, g, par):
                sp.wait_ge(fin_out, (l * NG + g) * FJ + FJ)
                sp.dma_start(u_dram[g], pix[par][:, :]).then_inc(u_stored[par], 16)

            load_weights(0)
            for s in range(2):
                if s == 0:
                    sp.wait_ge(t_done, TJ)
                sp.dma_start(v[s][4:7, :], grid).then_inc(x7_in[s], 16)
                sp.dma_start(v[s][0:4, :], x[s]).then_inc(x7_in[s], 16)
            with sp.Fori(0, HG - 1) as i:
                for par in range(2):
                    g = i * 2 + par
                    sp.wait_ge(v_used, g + 1)
                    sp.dma_start(v[par][0:4, :], x[g + 2]).then_inc(x7_in[par], 16)
                    store(0, g, par)
            for g in (NG - 2, NG - 1):
                store(0, g, g % 2)

            with sp.Fori(1, L) as l:
                for par in range(2):
                    sp.wait_ge(bd_ready, l * NCH + par - 1)
                    sp.dma_start(wd[par][:, :], fw[l * NCH + par]).then_inc(wd_in[par], 16)
                with sp.Fori(0, HG) as i:
                    for par in range(2):
                        sp.wait_ge(v_used, forward_use(l) + i * 2 + par - 1)
                        sp.wait_ge(u_stored[par], ((l - 1) * HG + i + 1) * 16)
                        sp.dma_start(v[par][:, :], u_dram[i * 2 + par]).then_inc(v_in[par], 16)
                load_weights(l * NCH)
                for par in range(2):
                    sp.wait_ge(v_used, inverse_use(l) + par - 1)
                    sp.dma_start(v[par][:, :], u_dram[par]).then_inc(v_in[par], 16)
                with sp.Fori(0, HG - 1) as i:
                    for par in range(2):
                        g = i * 2 + par
                        sp.wait_ge(v_used, inverse_use(l) + g + 1)
                        sp.dma_start(v[par][:, :], u_dram[g + 2]).then_inc(v_in[par], 16)
                        store(l, g, par)
                for g in (NG - 2, NG - 1):
                    store(l, g, g % 2)

            def load_last(i, par):
                if isinstance(i, int):
                    sp.wait_ge(v_used, FINAL_USE + par - 1)
                else:
                    sp.wait_ge(head_done, (i * 2 + par - 1) * FJ)
                sp.wait_ge(u_stored[par], ((L - 1) * HG + i + 1) * 16)
                sp.dma_start(v[par][:, :], u_dram[i * 2 + par]).then_inc(v_in[par], 16)

            def store_h(g, par):
                for s in range(2):
                    sp.wait_ge(head_out[s], (g + 1) * (FJ // 2))
                sp.dma_start(h_dram[g], pix[par][0:GI, :]).then_inc(h_stored[par], 16)

            for par in range(2):
                load_last(0, par)
            with sp.Fori(0, HG - 1) as i:
                for par in range(2):
                    load_last(i + 1, par)
                    store_h(i * 2 + par, par)
            for g in (NG - 2, NG - 1):
                store_h(g, g % 2)
            tok_sync(sp)

        @block.gpsimd
        def _(gp):
            def clear(l):
                if isinstance(l, int):
                    gp.wait_ge(f0_done, NF0 * F0J)
                else:
                    gp.wait_ge(fin_done, l * (NG * FJ))
                alone(gp)
                gp.memset(wide[:, :], 0.0).then_inc(bd_zero, 1)

            def take(l):
                gp.wait_ge(mix_out, (l + 1) * (NCH * MJ))
                alone(gp)

                def step(g, h, par):
                    reuse(gp, t3_done, T3J, l * NG + g)
                    src = spec_flat[:, bass.ds(g * (GI * SPEC), GI * SPEC)].rearrange("p (n m) -> p n m", m=2 * KX)
                    gp.tensor_copy(og16[par][:, :, 0, :], src).then_inc(og_hi, 1)
                    gp.wait_ge(og_hi, l * NG + g + 1)
                    alone(gp)
                    gp.tensor_tensor(og16[par][:, :, 1, :], src, og16[par][:, :, 0, :], ALU.subtract).then_inc(og_ready, 1)
                by_pairs(gp, l, NG, step)

            clear(0)
            take(0)
            with gp.Fori(1, L) as l:
                clear(l)
                take(l)
            tok_gpsimd(gp)

        @block.tensor
        def _(pe):
            def transposes(src, i):
                out = bank[i % 2][:, :].rearrange("p (x n) -> p x n", n=P)
                for q in range(4):
                    mm = pe.transpose(out[:, q, :], src[:, (4 * i + q) * P:(4 * i + q + 1) * P], idn[:, :])
                return mm

            def split_product(out, hi, lo, w):
                pe.matmul(out, hi, w[:, 0, :], start=True, stop=False)
                pe.matmul(out, hi, w[:, 1, :], start=False, stop=False)
                return pe.matmul(out, lo, w[:, 0, :], start=False, stop=True)

            def forward_y(par, i, pixels_used=False):
                out = bank[2 + i % 2][:, 0:8 * 48].rearrange("p (x m) -> p x m", m=48)
                for q in range(8):
                    x2 = slice((8 * i + q) * P, (8 * i + q + 1) * P)
                    mm = split_product(out[:, q, :], pix_hi[par][:, x2], pix_lo[par][:, x2], fy)
                    if q == 0 and pixels_used:
                        mm.then_inc(v_used, 1)
                mm.then_inc(y_done, 1)

            def forward_rows(par, i, flip):
                out = bank[4 + (flip + par + i) % 2][:, :].rearrange("p (k n) -> p k n", n=P)
                for q in range(4):
                    k = 4 * i + q
                    mm = pe.transpose(out[:, q, :], rowf[par][:, k * P:(k + 1) * P], idn[:, :])
                mm.then_inc(t2_done, 1)

            def forward_x(par, i):
                out = bank[6 + i][:, 0:6 * 48].rearrange("p (n m) -> p n m", m=48)
                for q in range(6):
                    n = 6 * i + q
                    b = slice(n * P, (n + 1) * P)
                    mm = split_product(out[:, q, :], rowt_hi[par][:, b], rowt_lo[par][:, b], fx)
                mm.then_inc(x_done, 1)

            def first_forward():
                pe.wait_ge(const_in, CONST)
                pe.wait_ge(x_in, 16)
                for i in range(TJ):
                    bank_free(pe, t_out, i)
                    transposes(v[0], i).then_inc(t_done, 1)
                for i in range(YJ):
                    pe.wait_ge(t_out, 2 * i + 2)
                    bank_free(pe, y_out, i)
                    forward_y(0, i)
                for i in range(T2J):
                    pe.wait_ge(y_out, YJ)
                    bank_free(pe, t2_out, i)
                    forward_rows(0, i, 0)
                for i in range(XJ):
                    pe.wait_ge(t2_out, T2J)
                    forward_x(0, i)
                pe.wait_ge(f0_const_in, 32)
                for q in range(NF0):
                    pe.wait_ge(f0_in[q % 2], 16 * KY4 * (q // 2 + 1))
                    for i in range(F0J):
                        n = q * F0J + i
                        if n >= 2:
                            pe.wait_ge(f0_out[n % 2], n // 2)
                        pe.matmul(bank[4 + n % 2][:, 0:384], p16_sb[:, :],
                                  f0_rows[q % 2][:, i * 384:(i + 1) * 384], start=True, stop=True)\
                          .then_inc(f0_done, 1)
                pe.sem_inc(t2_done, 1)
                pe.sem_inc(x_done, 1)

            def forward(l):
                def step(g, h, par, head, tail_):
                    a = (l - 1) * NG + g
                    k = forward_use(l) + g

                    def t(i):
                        if i % 2 == 0:
                            pe.wait_ge(relu_done, (k - NG) * 4 + i // 2 + 1)
                        bank_free(pe, t_out, (a + 1) * TJ + i)
                        transposes(v[par], i).then_inc(t_done, 1)

                    def y(i):
                        pe.wait_ge(t_out, (a + 1) * TJ + 2 * i + 2)
                        bank_free(pe, y_out, (a + 1) * YJ + i)
                        forward_y(par, i, i == 2)

                    def t2(i):
                        pe.wait_ge(y_out, (a - 1 + 1) * YJ + YJ)
                        bank_free(pe, t2_out, a * T2J + i)
                        forward_rows(1 - par, i, 1)

                    def xs(i):
                        pe.wait_ge(t2_out, a * T2J + T2J)
                        bank_free(pe, x_out, a * XJ + i)
                        forward_x(1 - par, i)

                    if head:
                        for i in range(4):
                            t(i)
                        y(0)
                        t(4), t(5)
                        y(1)
                        t(6), t(7)
                        y(2)
                    if tail_:
                        for i in range(T2J):
                            t2(i)
                    if head:
                        y(3)
                    if tail_:
                        for i in range(XJ):
                            xs(i)
                pipelined(pe, step)

            def mix(l):
                if isinstance(l, int):
                    for s in range(2):
                        pe.wait_ge(f0_out[s], NF0 * F0J // 2)
                else:
                    pe.wait_ge(x_out, (l * NG + 1) * XJ)
                alone(pe)

                def step(c, h, par):
                    m = l * NCH + c
                    pe.wait_ge(bd_ready, m + 1)
                    for i in range(MJ):
                        job = m * MJ + i
                        bank_free(pe, mix_out, job, MIX_BANKS)
                        acc = bank[(par * MJ + i) % MIX_BANKS][:, :].rearrange("p (m r b) -> p m r b", m=2, r=2)
                        for j in range(2):
                            w = bd[par][:, 2 * i + j]
                            at = (c * CH + (2 * i + j)) * 2
                            fr = spec[:, :, bass.ds(at, 1)].rearrange("p b m -> p (b m)")
                            fi = spec[:, :, bass.ds(at + 1, 1)].rearrange("p b m -> p (b m)")
                            pe.matmul(acc[:, j, 0, :], w[:, 0, :], fr, start=True, stop=False)
                            pe.matmul(acc[:, j, 0, :], w[:, 2, :], fi, start=False, stop=True)
                            pe.matmul(acc[:, j, 1, :], w[:, 1, :], fr, start=True, stop=False)
                            mm = pe.matmul(acc[:, j, 1, :], w[:, 0, :], fi, start=False, stop=True)
                        mm.then_inc(mix_done, 1)
                by_pairs(pe, l, NCH, step)

            def inverse(l):
                first = isinstance(l, int)
                pe.wait_ge(w7_ready if first else w_ready, 1 if first else l)

                def step(g, h, par, head, tail_):
                    n = l * NG + g
                    p0 = 1 - par

                    def t3(i):
                        pe.wait_ge(og_ready, n + 1)
                        bank_free(pe, t3_out, n * T3J + i)
                        alone(pe)
                        out = bank[(par + i) % 2][0:96, 0:256].bitcast(F16).rearrange("p (b n) -> p b n", n=P)
                        for j in range(GI):
                            mm = pe.transpose(out[:, j, :], og16[par][:, j * KYH + i].rearrange("p t m -> p (t m)"), idn16[:, :])
                        mm.then_inc(t3_done, 1)

                    def xi(i):
                        pe.wait_ge(t3_out, n * T3J + i + 1)
                        bank_free(pe, xi_out, n * XIJ + i)
                        out = bank[2 + (par + i) % 2][:, :].rearrange("p (k n) -> p k n", n=P)
                        for q in range(4):
                            k = 4 * i + q
                            rows = kxt[par][:, k * P:(k + 1) * P]
                            pe.matmul(out[:, q, :], rows, ix[:, 0, :], start=True, stop=False)
                            mm = pe.matmul(out[:, q, :], rows, ix[:, 1, :], start=False, stop=True)
                        mm.then_inc(xi_done, 1)

                    def t4(i):
                        pe.wait_ge(xi_out, (n + 1) * XIJ)
                        bank_free(pe, t4_out, n * T4J + i)
                        out = bank[4 + i % 2][0:96, :].rearrange("p (q n) -> p q n", n=P)
                        for q in range(4):
                            at = (4 * i + q) * 96
                            mm = pe.transpose(out[:, q, :], rowf[par][:, at:at + 96], idn[:, :])
                        mm.then_inc(t4_done, 1)

                    def final(i):
                        if first:
                            if i == 0:
                                pe.wait_ge(x7_in[p0], (half_before(h, par) + 2) * 16)
                        elif i % 2 == 0:
                            pe.wait_ge(relu_done, (inverse_use(l) + g - 1 - NG) * 4 + i // 2 + 1)
                        pe.wait_ge(t4_out, (n - 1) * T4J + i // 2 + 1)
                        bank_free(pe, fin_out, (n - 1) * FJ + i)
                        out = bank[6 + i % 2]
                        if first:
                            mm = pe.matmul(out[:, :], wx7[:, :], v[p0][0:7, i * 512:(i + 1) * 512], start=True, stop=False)
                        else:
                            mm = pe.matmul(out[:, :], wcur[:, :], v[p0][:, i * 512:(i + 1) * 512], start=True, stop=False)
                        if i == FJ - 1:
                            mm.then_inc(v_used, 1)
                        for q in range(2):
                            mm = pe.matmul(out[:, q * 256:(q + 1) * 256], ht[p0][:, 2 * i + q, :], iy[:, :],
                                           start=False, stop=(q == 1))
                        mm.then_inc(fin_done, 1)

                    inverse_order(head, tail_, t3=t3, xi=xi, t4=t4, final=final)
                pipelined(pe, step, first)

            def average(l):
                pe.wait_ge(bn_step, l * BN_STEPS + 3)
                pe.matmul(bank[0][:, 0:2], avg_sb[:, :], bn[:, 2:4], start=True, stop=True).then_inc(bn_avg, 1)

            def layer0_weights():
                pe.wait_ge(mix_out, NCH * MJ)
                pe.matmul(bank[2][0:7, 0:P], pt7_sb[:, :], wm[:, 0, :], start=True, stop=True).then_inc(w7_done, 1)

            first_forward()
            mix(0)
            layer0_weights()
            inverse(0)
            average(0)
            with pe.Fori(1, L) as l:
                forward(l)
                mix(l)
                inverse(l)
                average(l)

            pe.wait_ge(q_step, 1)
            pe.matmul(bank[4][:, 0:1], quarter_sb[:, :], bn[:, 22:23], start=True, stop=True).then_inc(q_sum, 1)
            pe.wait_ge(q_ready, 1)

            def step(g, h, par, head, tail_):
                if head:
                    pe.wait_ge(v_in[par], ((L - 1) * NG + h + 1) * 16)
                    for i in range(FJ):
                        if not isinstance(g, int) or g >= 1:
                            pe.wait_ge(head_out[i % 2], g * (FJ // 2) - (FJ // 2 - 1) + i // 2)
                        pe.matmul(bank[i][0:GI, :], qcol[:, :], v[par][:, i * 512:(i + 1) * 512], start=True, stop=True)\
                          .then_inc(head_done, 1)
            pipelined(pe, step, True)
            tok_tensor(pe)

        @block.scalar
        def _(act):
            def first_forward():
                act.wait_ge(const_in, CONST)
                for i in range(TJ):
                    act.wait_ge(t_done, i + 1)
                    rows_hi(0, i)
                for i in range(YJ):
                    act.wait_ge(y_done, i + 1)
                    columns_out(0, i).then_inc(y_out, 1)
                for i in range(XJ):
                    act.wait_ge(x_done, i + 1)
                    act.copy(og[0][:, i * 288:(i + 1) * 288], bank[6 + i][:, 0:288]).then_inc(x_out, 1)
                for n in range(0, NF0 * F0J, 2):
                    act.wait_ge(f0_done, n + 1)
                    act.copy(spec_flat[:, n * 384:(n + 1) * 384], bank[4][:, 0:384]).then_inc(f0_out[0], 1)

            def rows_hi(par, i):
                act.copy(pix_hi[par][:, i * 512:(i + 1) * 512], bank[i % 2][:, :]).then_inc(t_hi, 1)

            def columns_out(par, i):
                dst = rowf[par][:, :].rearrange("p (k x r) -> p x k r", k=M2, r=2)[:, 16 * i:16 * i + 16]
                src = bank[2 + i % 2][:, 0:384].rearrange("p (x k r) -> p x k r", k=M2, r=2)
                return act.copy(dst, src)

            def activate(half, par, quarters=range(4)):
                act.wait_ge(v_in[par], (half + 1) * 16)
                for i in quarters:
                    px = v[par][:, i * 1024:(i + 1) * 1024]
                    act.activation(px, px, ACT.Relu, bias=bias_l, scale=scale_l).then_inc(relu_done, 1)

            def forward(l):
                act.wait_ge(bn_step, l * BN_STEPS)
                act.wait_ge(og_ready, l * NG)
                for s in range(2):
                    act.wait_ge(u_stored[s], l * HG * 16)
                activate((l - 1) * NG, 0)

                def step(g, h, par, head, tail_):
                    a = (l - 1) * NG + g
                    if head:
                        act.wait_ge(y_done, a * YJ + 1)
                        act.wait_ge(t2_done, a * T2J + 1)
                        for i in range(YJ):
                            for j in (2 * i, 2 * i + 1):
                                act.wait_ge(t_done, (a + 1) * TJ + j + 1)
                                rows_hi(par, j)
                            if i:
                                act.wait_ge(y_done, (a + 1) * YJ + i)
                                columns_out(par, i - 1).then_inc(y_out, 1)
                            if not isinstance(g, int) or g < NG - 1:
                                activate((l - 1) * NG + h + par, 1 - par, (i,))
                        act.wait_ge(y_done, (a + 1) * YJ + 4)
                        columns_out(par, 3).then_inc(y_out, 1)
                    if tail_:
                        for i in range(XJ):
                            act.wait_ge(x_done, a * XJ + i + 2)
                            act.copy(spec_flat[:, bass.ds((g - 1) * (GI * SPEC) + i * 288, 288)], bank[6 + i][:, 0:288])\
                               .then_inc(x_out, 1)
                pipelined(act, step)

            def mix(l):
                def step(c, h, par):
                    for i in range(MJ):
                        act.wait_ge(mix_done, (l * NCH + c) * MJ + i + 1)
                        src = bank[(par * MJ + i) % MIX_BANKS][:, :].rearrange("p (m b) -> p m b", b=B)
                        dst = spec[:, :, bass.ds((c * CH + 2 * i) * 2, 4)].rearrange("p b m -> p m b")
                        act.copy(dst, src).then_inc(mix_out, 1)
                by_pairs(act, l, NCH, step)

            def inverse(l):
                first = isinstance(l, int)
                act.wait_ge(w7_ready if first else w_ready, 1 if first else l)

                def step(g, h, par, head, tail_):
                    n = l * NG + g
                    p0 = 1 - par

                    def final(i):
                        act.wait_ge(fin_done, (n - 1) * FJ + i + 1)
                        act.activation(pix[p0][:, i * 512:(i + 1) * 512], bank[6 + i % 2][:, :], ACT.Identity, bias=wb)\
                           .then_inc(fin_out, 1)

                    def final_and_next(i):
                        final(i)
                        if i >= 4:
                            next_pixels(i - 4)

                    def next_pixels(i):
                        if head and not first:
                            activate((l - 1) * NG + HG + h, par, (i,))

                    def xi(i):
                        act.wait_ge(xi_done, n * XIJ + i + 1)
                        dst = rowf[par][:, :].rearrange("p (x k r) -> p k x r", k=M2, r=2)[:, 4 * i:4 * i + 4]
                        src = bank[2 + (par + i) % 2][:, :].rearrange("p (k x r) -> p k x r", k=4, r=2)
                        act.copy(dst, src).then_inc(xi_out, 1)

                    if tail_:
                        if not isinstance(n, int) or n >= 3:
                            act.wait_ge(stats_done, (n - 2) * FJ)
                            act.wait_ge(u_stored[p0], (l * HG + half_before(h, par)) * 16)
                    if head:
                        reuse(act, t4_done, T4J, n)
                    inverse_order(head, tail_, xi=xi, final=final_and_next)
                    if not tail_:
                        for i in range(4):
                            next_pixels(i)
                pipelined(act, step, first)

            def deviation(l):
                act.wait_ge(bn_step, l * BN_STEPS + 6)
                act.activation(bn[:, 9:10], bn[:, 8:9], ACT.Sqrt).then_inc(bn_sqrt, 1)

            first_forward()
            mix(0)
            inverse(0)
            deviation(0)
            with act.Fori(1, L) as l:
                forward(l)
                mix(l)
                inverse(l)
                deviation(l)

            act.wait_ge(q_ready, 1)

            for q in range(2):
                act.wait_ge(u_stored[q], L * HG * 16)

            def step(g, h, par, head, tail_):
                if head:
                    if not isinstance(g, int) or g >= 2:
                        act.wait_ge(h_stored[par], h * 16)
                    for i in range(0, FJ, 2):
                        act.wait_ge(head_done, g * FJ + i + 1)
                        act.activation(pix[par][0:GI, i * 512:(i + 1) * 512], bank[i][0:GI, :], ACT.Identity,
                                       bias=hconst[0:GI, :]).then_inc(head_out[0], 1)
            pipelined(act, step, True)
            tok_scalar(act)

        @block.vector
        def _(dve):
            def rows_lo(par, i):
                px = slice(i * 512, (i + 1) * 512)
                dve.tensor_tensor(pix_lo[par][:, px], bank[i % 2][:, :], pix_hi[par][:, px], ALU.subtract).then_inc(t_out, 1)

            def first_forward():
                dve.wait_ge(const_in, CONST)
                for i in range(TJ):
                    dve.wait_ge(t_hi, i + 1)
                    rows_lo(0, i)
                for i in range(T2J):
                    dve.wait_ge(t2_done, i + 1)
                    b = slice(i * 512, (i + 1) * 512)
                    dve.tensor_copy(rowt_hi[0][:, b], bank[4 + i % 2][:, :]).then_inc(t2_hi, 1)
                    dve.wait_ge(t2_hi, i + 1)
                    dve.tensor_tensor(rowt_lo[0][:, b], bank[4 + i % 2][:, :], rowt_hi[0][:, b], ALU.subtract).then_inc(t2_out, 1)
                for n in range(1, NF0 * F0J, 2):
                    dve.wait_ge(f0_done, n + 1)
                    dve.tensor_copy(spec_flat[:, n * 384:(n + 1) * 384], bank[5][:, 0:384]).then_inc(f0_out[1], 1)

            def forward(l):
                for s in range(2):
                    dve.wait_ge(u_stored[s], l * HG * 16)

                def step(g, h, par, head, tail_):
                    a = (l - 1) * NG + g
                    if head:
                        dve.wait_ge(y_done, a * YJ + 1)
                        for i in range(TJ):
                            dve.wait_ge(t_hi, (a + 1) * TJ + i + 1)
                            rows_lo(par, i)
                    if tail_:
                        p0 = 1 - par
                        dve.wait_ge(x_done, (a - 1) * XJ + 1)
                        for i in range(T2J):
                            dve.wait_ge(t2_done, a * T2J + i + 2)
                            hi, lo = (t[p0].rearrange("p (b k c) -> p k b c", k=M2, c=C)[:, 4 * i:4 * i + 4]
                                      for t in (rowt_hi, rowt_lo))
                            src = bank[4 + (1 + p0 + i) % 2][:, :].rearrange("p (k b c) -> p k b c", k=4, c=C)
                            dve.tensor_copy(hi, src).then_inc(t2_hi, 1)
                            dve.wait_ge(t2_hi, a * T2J + i + 1)
                            dve.tensor_tensor(lo, src, hi, ALU.subtract).then_inc(t2_out, 1)
                pipelined(dve, step)

            def mix_weights(l):
                dve.wait_ge(bd_zero, l + 1)
                alone(dve)

                def step(c, h, par):
                    m = l * NCH + c
                    dve.wait_ge(wd_in[par], (l * (NCH // 2) + h + 1) * 16)
                    reuse(dve, mix_done, MJ, m)
                    for j in range(KY4):
                        r = slice(j * C, (j + 1) * C)
                        dve.tensor_copy(bd[par][r, :, 0:2, j * C:(j + 1) * C], wds[par][r, :, :, :])
                        ins = dve.tensor_scalar(bd[par][r, :, 2, j * C:(j + 1) * C], wds[par][r, :, 1, :], -1.0, None, ALU.mult)
                    ins.then_inc(bd_ready, 1)
                by_pairs(dve, l, NCH, step)

            def inverse(l):
                def step(g, h, par, head, tail_):
                    n = l * NG + g
                    p0 = 1 - par

                    def count(i):
                        dve.wait_ge(fin_out, (n - 1) * FJ + i + 1)
                        dve.bn_stats(stats[:, bass.ds((g - 1) * (FJ * 6) + i * 6, 6)], pix[p0][:, i * 512:(i + 1) * 512])\
                           .then_inc(stats_done, 1)

                    def t3(i):
                        dve.wait_ge(t3_done, n * T3J + i + 1)
                        dst = kxt[par][:, i * 512:(i + 1) * 512].rearrange("p (k b o) -> p b k o", k=4, o=C)
                        src = bank[(par + i) % 2][0:96, 0:256].bitcast(F16).rearrange("p (b k o) -> p b k o", k=4, o=C)
                        dve.tensor_copy(dst, src).then_inc(t3_out, 1)

                    def t4(i):
                        dve.wait_ge(t4_done, n * T4J + i + 1)
                        dve.tensor_copy(ht[par][:, 4 * i:4 * i + 4, :].rearrange("p q n -> p (q n)"), bank[4 + i % 2][0:96, :])\
                           .then_inc(t4_out, 1)

                    if head:
                        reuse(dve, xi_done, XIJ, n)
                        reuse(dve, fin_done, FJ, n)
                    inverse_order(head, tail_, t3=t3, t4=t4, final=count)
                pipelined(dve, step, isinstance(l, int))

            def normalise(l):
                base = l * BN_STEPS
                done = [0]

                def step(ins):
                    done[0] += 1
                    ins.then_inc(bn_step, 1)
                    dve.wait_ge(bn_step, base + done[0])

                dve.wait_ge(stats_done, (l + 1) * (NG * FJ))
                alone(dve)
                step(dve.bn_aggr(bn[:, 0:2], stats[:, :]))
                step(dve.tensor_copy(bn[:, 2:3], bn[:, 0:1]))
                step(dve.scalar_tensor_tensor(bn[:, 3:4], bn[:, 0:1], bn[:, 0:1], bn[:, 1:2], ALU.mult, ALU.add))
                dve.wait_ge(bn_avg, l + 1)
                step(dve.tensor_copy(bn[:, 4:6], bank[0][:, 0:2]))
                step(dve.scalar_tensor_tensor(bn[:, 7:8], bn[:, 4:5], bn[:, 4:5], bn[:, 5:6], ALU.mult, ALU.subtract))
                step(dve.tensor_scalar(bn[:, 8:9], bn[:, 7:8], -1.0, EPS, ALU.mult, ALU.add))
                dve.wait_ge(bn_sqrt, l + 1)
                step(dve.reciprocal(bn[:, 10:11], bn[:, 9:10]))
                step(dve.scalar_tensor_tensor(bn[:, 11:12], bn[:, 10:11], bn[:, 10:11], bn[:, 8:9], ALU.mult, ALU.mult))
                step(dve.tensor_scalar(bn[:, 12:13], bn[:, 11:12], -0.5, 1.5, ALU.mult, ALU.add))
                step(dve.tensor_tensor(bn[:, 13:14], bn[:, 10:11], bn[:, 12:13], ALU.mult))
                step(dve.tensor_tensor(scale_l, bn[:, 13:14], gamma, ALU.mult))
                step(dve.scalar_tensor_tensor(bn[:, 14:15], bn[:, 4:5], scale_l, beta, ALU.mult, ALU.subtract))
                step(dve.tensor_scalar(bias_l, bn[:, 14:15], -1.0, None, ALU.mult))
                assert done[0] == BN_STEPS

            def layer_constants(l):
                dve.tensor_copy(wcur[:, :], wm[:, l, :])
                dve.tensor_copy(bn[:, 18:20], chan_sb[:, l, 1:3])
                dve.tensor_copy(wb, chan_sb[:, l, 0:1]).then_inc(w_ready, 1)

            first_forward()
            dve.tensor_copy(bn[:, 18:20], chan_sb[:, 0, 1:3])
            dve.tensor_copy(wb, chan_sb[:, 0, 0:1])
            mix_weights(0)
            dve.wait_ge(w7_done, 1)
            dve.tensor_copy(wx7[:, :], bank[2][0:7, 0:P]).then_inc(w7_ready, 1)
            inverse(0)
            normalise(0)
            with dve.Fori(1, L) as l:
                forward(l)
                layer_constants(l)
                mix_weights(l)
                inverse(l)
                normalise(l)

            dve.tensor_scalar(bn[:, 22:23], qbd_sb[:, GI:GI + 1], bias_l, None, ALU.mult).then_inc(q_step, 1)
            dve.wait_ge(q_sum, 1)
            dve.tensor_scalar(hconst, bank[4][:, 0:1], qb_sb[:, 0:1], None, ALU.add)
            dve.tensor_scalar(qcol[:, :], qbd_sb[:, 0:GI], scale_l, None, ALU.mult).then_inc(q_ready, 1)

            for q in range(2):
                dve.wait_ge(u_stored[q], L * HG * 16)

            def step(g, h, par, head, tail_):
                if head:
                    if not isinstance(g, int) or g >= 2:
                        dve.wait_ge(h_stored[par], h * 16)
                    for i in range(1, FJ, 2):
                        dve.wait_ge(head_done, g * FJ + i + 1)
                        dve.tensor_scalar(pix[par][0:GI, i * 512:(i + 1) * 512], bank[i][0:GI, :], hconst[0:GI, :],
                                          None, ALU.add).then_inc(head_out[1], 1)
            pipelined(dve, step, True)
            tok_vector(dve)

NTOK = B * S
NT = NTOK // P
D = S
H, HD = 8, 8
WS2 = 49
PAD = S - WS2
TAB = 13 * 13
NIDX = WS2 * WS2
NE, FF = 16, 128
NI = NT // 2
EH = NE // 2
LN_STEPS = 10


def three_stages(eng, step):
    step(0, 0, (True, False, False))
    step(1, 1, (True, True, False))
    step(2, 0, (True, True, True))
    step(3, 1, (True, True, True))
    with eng.Fori(2, NT // 2) as i:
        step(i * 2, 0, (True, True, True))
        step(i * 2 + 1, 1, (True, True, True))
    step(NT, 0, (False, True, True))
    step(NT + 1, 1, (False, False, True))


def token_programs(nc, ctx, bank, sem, h_dram, h_stored, att, moe, out):
    bias_dram = nc.dram_tensor("rel_bias", [H, WS2, WS2], F32, kind="Internal").ap()

    def pair(name):
        return [sem(f"{name}{s}") for s in range(2)]

    def sb(name, shape, dt=F32):
        return ctx.enter_context(nc.sbuf_tensor(name, shape, dt))

    consts = []

    def const(name, src):
        t = sb(name, list(src.shape))
        consts.append((t, src))
        return t

    h = sb("h", [P, NT, D])
    xn = sb("xn", [P, NT, D])
    sq = sb("sq", [P, NT, D])
    ln = sb("ln", [P, 8, NT])
    idn = const("t_ident", att["ident"])
    wqk = const("wqk", att["wqk"])
    wv = const("wv", att["wv"])
    wp = const("wp", att["wp"])
    head_mask = const("head_mask", att["head_mask"])
    v_mask = const("v_mask", att["v_mask"])
    iota = const("iota", att["iota"])
    tab = [const("tab0", att["table"][0:P, :]), const("tab1", att["table"][P:TAB, :])]
    gw = const("gw", moe["gw"])
    w1 = const("w1", moe["w1"])
    w2 = const("w2", moe["w2"])
    b2 = const("b2", moe["b2"])
    gamma = const("gamma", moe["gamma"])
    beta = const("beta", moe["beta"])
    erow = const("erow", moe["erow"])
    idx = sb("idx", [P, NIDX], I32)
    idxf = sb("idxf", [P, NIDX])
    hot = [sb(f"hot{s}", [P, NIDX]) for s in range(2)]
    bias_rows = sb("bias_rows", [H, NIDX])
    bias = sb("bias", [P, H, S])
    xc = [sb(f"xc{s}", [P, D]) for s in range(2)]
    xT = [sb(f"xT{s}", [D, 2, 2, S]) for s in range(2)]
    qd = [sb(f"qd{s}", [P, P]) for s in range(2)]
    ks = [sb(f"ks{s}", [P, S]) for s in range(2)]
    kd = [sb(f"kd{s}", [P, H, S]) for s in range(2)]
    vd = [sb(f"vd{s}", [P, 2, D]) for s in range(2)]
    sc = [sb(f"sc{s}", [P, H, S]) for s in range(2)]
    mx = [sb(f"mx{s}", [P, H]) for s in range(2)]
    sm = [sb(f"sm{s}", [P, H]) for s in range(2)]
    rs = [sb(f"rs{s}", [P, H]) for s in range(2)]
    pT = [sb(f"pT{s}", [P, 4, P]) for s in range(2)]
    o = [sb(f"o{s}", [P, D]) for s in range(2)]
    oT = [sb(f"oT{s}", [D + 1, P]) for s in range(2)]
    xTa = sb("xTa", [D + 1, NTOK])
    lg = sb("lg", [P, NT, NE])
    top = sb("top", [P, NT, 8])
    topi = sb("topi", [P, NT, 8], U32)
    gv = sb("gv", [P, 6, NT])
    gate = sb("gate", [P, NT, NE])
    gate2 = sb("gate2", [P, NT, NE])
    gT = sb("gT", [P, NT // 8, P])
    hid = [sb(f"hid{s}", [P, 2, 2 * P]) for s in range(4)]
    wo = [sb(f"wo{s}", [P, 2, EH * D]) for s in range(2)]

    c_in, idx_in, h_in, out_st = sem("c_in"), sem("idx_in"), sem("h_in"), sem("out_st")
    cleared, t_waited = sem("cleared"), sem("t_waited")
    ln_step, ln_sq, ln_sqrt = sem("ln_step"), sem("ln_sq"), sem("ln_sqrt")
    hot_ready, rb_done, rb_out, rb_stored, bias_in = (sem("hot_ready"), sem("rb_done"), sem("rb_out"),
                                                      sem("rb_stored"), sem("bias_in"))
    xc_ready, xt_done, xt_out = sem("xc_ready"), sem("xt_done"), sem("xt_out")
    qk_done, qk_out, kd_ready = sem("qk_done"), sem("qk_out"), sem("kd_ready")
    v_done, v_out = sem("v_done"), sem("v_out")
    s_done, s_out, mx_done, sub_done, exp_done, sum_done, rs_done = (
        sem("s_done"), sem("s_out"), sem("mx_done"), sem("sub_done"), sem("exp_done"), sem("sum_done"), sem("rs_done"))
    pt_done, pt_out, av_done, o_out = sem("pt_done"), sem("pt_out"), sem("av_done"), sem("o_out")
    ot_done, ot_out, pr_done, pr_out = sem("ot_done"), sem("ot_out"), sem("pr_done"), sem("pr_out")
    x_ready, mt_done, mt_out, lg_done, lg_out = (sem("x_ready"), sem("mt_done"), sem("mt_out"), sem("lg_done"),
                                                 sem("lg_out"))
    top_done, gap_ready, gap_exp, gate_step = sem("top_done"), sem("gap_ready"), sem("gap_exp"), sem("gate_step")
    gt_done, gt_out, b2_done, b2_out = sem("gt_done"), sem("gt_out"), sem("b2_done"), sem("b2_out")
    hid_done, hid_out, hid_used = sem("hid_done"), pair("hid_out"), sem("hid_used")
    eo_done, eo_out, sum_step, moe_sum = sem("eo_done"), sem("eo_out"), sem("sum_step"), sem("moe_sum")
    fin_step = sem("fin_step")
    C_IN = 16 * len(consts)
    GATE_STEPS, FIN_STEPS = 8, 4
    NCLEAR = 6
    HJ = 8
    RB = [(i * 512, min(512, NIDX - i * 512)) for i in range(-(-NIDX // 512))]

    def apart(eng):
        eng.sem_inc(t_waited, 1)

    def tile(t3, t):
        return t3[:, bass.ds(t, 1), :].rearrange("p t y -> p (t y)")

    def sync(sp):
        for s in range(2):
            sp.wait_ge(h_stored[s], 16 * HG)
        for t, src in consts:
            sp.dma_start(t[:], src).then_inc(c_in, 16)
        sp.dma_start(idx[:, :], att["index"].broadcast_to([P, NIDX])).then_inc(idx_in, 16)
        sp.dma_start(h[:, :, :], h_dram.rearrange("g i (n y) -> (g i n) y", y=D).rearrange("(t p) y -> p t y", p=P))\
          .then_inc(h_in, 16)
        sp.wait_ge(rb_out, len(RB))
        sp.dma_start(bias_dram.rearrange("h n m -> h (n m)"), bias_rows[:, :]).then_inc(rb_stored, 16)
        sp.wait_ge(rb_stored, 16)
        sp.wait_ge(cleared, NCLEAR)
        for i in range(2):
            sp.dma_start(bias[i * S + PAD:(i + 1) * S, :, PAD:S], bias_dram.rearrange("h n m -> n h m")).then_inc(bias_in, 16)
        sp.wait_ge(fin_step, FIN_STEPS + 1)
        sp.dma_start(out.rearrange("b n y -> (b n) y").rearrange("(t p) y -> p t y", p=P), h[:, :, :]).then_inc(out_st, 16)
        sp.wait_ge(out_st, 16)

    def gpsimd(gp):
        for s in range(2):
            gp.wait_ge(h_stored[s], 16 * HG)
        gp.memset(bias[:, :, :], 0.0).then_inc(cleared, 1)
        for s in range(2):
            gp.memset(qd[s][:, :], 0.0).then_inc(cleared, 1)
            gp.memset(oT[s][:, :], 1.0).then_inc(cleared, 1)
        gp.memset(xTa[:, :], 1.0).then_inc(cleared, 1)
        gp.wait_ge(c_in, C_IN)

        def step(t, par, on):
            if on[0]:
                gp.wait_ge(qk_out, (t + 1) * 2)
                reuse(gp, s_done, 1, t)
                gp.tensor_tensor(kd[par][:, :, :], ks[par][:, :].unsqueeze(1).to_broadcast([P, H, S]),
                                 head_mask[:, :].unsqueeze(2).to_broadcast([P, H, S]), ALU.mult).then_inc(kd_ready, 1)
            if on[1]:
                p1 = 1 - par
                gp.wait_ge(mx_done, t)
                gp.tensor_tensor(sc[p1][:, :, :], sc[p1][:, :, :], mx[p1][:, :].unsqueeze(2).to_broadcast([P, H, S]),
                                 ALU.subtract).then_inc(sub_done, 1)
        three_stages(gp, step)

        def turn(it):
            for q in range(2):
                n = it * 2 + q
                w = wo[q][:, :, :].rearrange("p a n -> p (a n)")
                gp.wait_ge(eo_out, it * 4 + 3 + q)
                width = NE * D // 2
                done = 0
                while width > D:
                    gp.tensor_tensor(w[:, 0:width], w[:, 0:width], w[:, width:2 * width], ALU.add).then_inc(sum_step, 1)
                    done += 1
                    gp.wait_ge(sum_step, n * 3 + done)
                    width //= 2
                gp.tensor_tensor(tile(sq, n), w[:, 0:D], w[:, D:2 * D], ALU.add).then_inc(moe_sum, 1)
        with gp.Fori(0, NI) as it:
            turn(it)

    def tensor(pe):
        pe.wait_ge(c_in, C_IN)
        pe.wait_ge(hot_ready, 2)
        for i, (at, n) in enumerate(RB):
            bank_free(pe, rb_out, i)
            pe.matmul(bank[i % 2][0:H, 0:n], tab[0][:, :], hot[0][:, at:at + n], start=True, stop=False)
            pe.matmul(bank[i % 2][0:H, 0:n], tab[1][:, :], hot[1][0:TAB - P, at:at + n], start=False, stop=True)\
              .then_inc(rb_done, 1)
        pe.wait_ge(rb_out, len(RB))
        pe.wait_ge(cleared, NCLEAR)

        def step(t, par, on):
            a, b, c = on
            p1 = 1 - par

            def features():
                pe.wait_ge(xc_ready, t + 1)
                bank_free(pe, xt_out, t, 1)
                apart(pe)
                pe.transpose(bank[0][0:D, 0:P], xc[par][:, :], idn[:, :]).then_inc(xt_done, 1)

            def projections():
                pe.wait_ge(xt_out, t + 1)
                bank_free(pe, qk_out, t * 2, 1)
                rhs = xT[par][:, :, 0, :]
                pe.matmul(bank[1][:, 0:P], wqk[:, 0:P], rhs, start=True, stop=True)
                pe.matmul(bank[1][:, P:2 * P], wqk[:, P:2 * P], rhs, start=True, stop=True).then_inc(qk_done, 1)
                bank_free(pe, v_out, t, 1)
                for i in range(2):
                    mm = pe.matmul(bank[2][:, i * D:(i + 1) * D], xT[par][:, i, :, :].rearrange("p c n -> p (c n)"),
                                   wv[:, :], start=True, stop=True)
                mm.then_inc(v_done, 1)

            def scores():
                pe.wait_ge(kd_ready, t)
                bank_free(pe, s_out, t - 1, 1)
                pe.matmul(bank[3][:, :], qd[p1][:, :], kd[p1][:, :, :].rearrange("p h m -> p (h m)"),
                          start=True, stop=True).then_inc(s_done, 1)

            def turned():
                pe.wait_ge(exp_done, t - 1)
                bank_free(pe, pt_out, t - 2, 1)
                for i in range(4):
                    mm = pe.transpose(bank[4][:, i * P:(i + 1) * P], sc[par][:, 2 * i:2 * i + 2, :].rearrange("p h m -> p (h m)"),
                                      idn[:, :])
                mm.then_inc(pt_done, 1)

            def values():
                pe.wait_ge(pt_out, t - 1)
                pe.wait_ge(v_out, t - 1)
                bank_free(pe, o_out, t - 2, 1)
                for i in range(2):
                    for j in range(4):
                        mm = pe.matmul(bank[5][i * S:(i + 1) * S, j * 16:(j + 1) * 16], pT[par][:, j, i * S:(i + 1) * S],
                                       vd[par][:, i, j * 16:(j + 1) * 16], start=True, stop=True)
                mm.then_inc(av_done, 1)

            def joined():
                pe.wait_ge(o_out, t - 1)
                bank_free(pe, ot_out, t - 2, 1)
                apart(pe)
                pe.transpose(bank[6][0:D, 0:P], o[par][:, :], idn[:, :]).then_inc(ot_done, 1)

            def projected():
                pe.wait_ge(ot_out, t - 1)
                bank_free(pe, pr_out, t - 2, 1)
                pe.matmul(bank[7][:, 0:D], oT[par][:, :], wp[:, :], start=True, stop=True).then_inc(pr_done, 1)

            if a:
                features()
            if c:
                turned()
            if a:
                projections()
            if c:
                values()
            if b:
                scores()
            if c:
                joined()
                projected()
        three_stages(pe, step)

        pe.wait_ge(x_ready, 1)
        for t in range(NT):
            n, q = divmod(t, 4)
            if q == 0:
                bank_free(pe, mt_out, n)
            mm = pe.transpose(bank[n % 2][0:D, q * P:(q + 1) * P], xn[:, t, :], idn[:, :])
            if q == 3:
                mm.then_inc(mt_done, 1)
                if n % 2:
                    pe.wait_ge(mt_out, n + 1)
                    bank_free(pe, lg_out, n // 2)
                    for r in range(8):
                        tt = t - 7 + r
                        mm = pe.matmul(bank[2 + n // 2 % 2][:, r * NE:(r + 1) * NE], xTa[:, tt * P:(tt + 1) * P], gw[:, :],
                                       start=True, stop=True)
                    mm.then_inc(lg_done, 1)
        pe.wait_ge(gate_step, GATE_STEPS)
        for n in range(NT // 8):
            bank_free(pe, gt_out, n)
            pe.transpose(bank[4 + n % 2][:, 0:P], gate[:, 8 * n:8 * n + 8, :].rearrange("p t e -> p (t e)"), idn[:, :])\
              .then_inc(gt_done, 1)
            pe.wait_ge(gt_out, n + 1)
            bank_free(pe, b2_out, n)
            pe.matmul(bank[6 + n % 2][:, :], gT[:, n, :], b2[:, :], start=True, stop=True).then_inc(b2_done, 1)
        pe.wait_ge(b2_out, NT // 8)

        def turn(it):
            now = not isinstance(it, int)

            def hidden(j):
                if now or j >= 4:
                    pe.wait_ge(hid_out[j % 2], it * (HJ // 2) + j // 2 - 1)
                for i in range(2):
                    e = 2 * j + i
                    mm = pe.matmul(bank[j % 4][:, i * 2 * P:(i + 1) * 2 * P], w1[:, e * FF:(e + 1) * FF],
                                   xTa[:, bass.ds(it * (2 * P), 2 * P)], start=True, stop=True)
                mm.then_inc(hid_done, 1)

            def output(j):
                half = j // 4
                if j % 4 == 0 and now:
                    pe.wait_ge(eo_out, it * 4 - 2 + 2 * half)
                pe.wait_ge(hid_out[j % 2], it * (HJ // 2) + j // 2 + 1)
                for i in range(2):
                    e = 2 * j + i
                    for q in range(2):
                        mm = pe.matmul(bank[4 + 2 * half + q][:, (e % EH) * D:(e % EH + 1) * D],
                                       hid[j % 4][:, i, q * P:(q + 1) * P], w2[:, e * D:(e + 1) * D], start=True, stop=True)
                mm.then_inc(hid_used, 1)

            hidden(0), hidden(1), hidden(2)
            for j in range(HJ):
                output(j)
                if j + 3 < HJ:
                    hidden(j + 3)
        turn(0)
        with pe.Fori(1, NI) as it:
            turn(it)

    def layer_norm_act(act, use):
        act.wait_ge(ln_step, use * LN_STEPS + 3)
        act.activation(sq[:, :, :], xn[:, :, :], ACT.Square).then_inc(ln_sq, 1)
        act.wait_ge(ln_step, use * LN_STEPS + 5)
        act.activation(ln[:, 3, :], ln[:, 2, :], ACT.Sqrt).then_inc(ln_sqrt, 1)

    def scalar(act):
        act.wait_ge(c_in, C_IN)
        for i, (at, n) in enumerate(RB):
            act.wait_ge(rb_done, i + 1)
            act.copy(bias_rows[:, at:at + n], bank[i % 2][0:H, 0:n]).then_inc(rb_out, 1)
        layer_norm_act(act, 0)
        act.wait_ge(ln_step, LN_STEPS)
        act.wait_ge(cleared, NCLEAR)

        def step(t, par, on):
            a, b, c = on
            p1 = 1 - par
            if a:
                reuse(act, xt_done, 1, t)
                act.activation(xc[par][:, :], tile(xn, t), ACT.Copy, scale=ln[:, 7, bass.ds(t, 1)]).then_inc(xc_ready, 1)
            if c:
                act.wait_ge(pt_done, t - 1)
                reuse(act, av_done, 1, t - 2)
                act.copy(pT[par][:, :, :].rearrange("p i n -> p (i n)"), bank[4][:, :]).then_inc(pt_out, 1)
            if a:
                act.wait_ge(xt_done, t + 1)
                reuse(act, v_done, 1, t)
                act.copy(xT[par][:, :, :, :],
                         bank[0][0:D, 0:P].rearrange("p (i n) -> p i n", i=2).unsqueeze(2).to_broadcast([D, 2, 2, S]))\
                   .then_inc(xt_out, 1)
                act.wait_ge(qk_done, t + 1)
                reuse(act, s_done, 1, t)
                for i in range(2):
                    r = slice(i * D, (i + 1) * D)
                    act.copy(qd[par][r, i * S:(i + 1) * S], bank[1][r, i * S:(i + 1) * S])
                    ins = act.copy(ks[par][r, :], bank[1][r, P + i * S:P + (i + 1) * S])
                    ins.then_inc(qk_out, 1)
            if b:
                act.wait_ge(sub_done, t)
                px = sc[p1][:, :, :]
                act.activation(px, px, ACT.Exp).then_inc(exp_done, 1)
            if c:
                act.wait_ge(ot_done, t - 1)
                reuse(act, pr_done, 1, t - 2)
                act.copy(oT[par][0:D, :], bank[6][0:D, 0:P]).then_inc(ot_out, 1)
        three_stages(act, step)

        layer_norm_act(act, 1)
        for n in range(NT // 4):
            act.wait_ge(mt_done, n + 1)
            act.copy(xTa[0:D, n * 512:(n + 1) * 512], bank[n % 2][0:D, :]).then_inc(mt_out, 1)
        act.wait_ge(gap_ready, 1)
        act.activation(gv[:, 1, :], gv[:, 0, :], ACT.Exp).then_inc(gap_exp, 1)

        def turn(it):
            for j in range(0, HJ, 2):
                act.wait_ge(hid_done, it * HJ + j + 1)
                if not isinstance(it, int) or j >= 4:
                    act.wait_ge(hid_used, it * HJ + j - 3)
                act.activation(hid[j % 4][:, :, :].rearrange("p i n -> p (i n)"), bank[j % 4][:, :], ACT.Relu)\
                   .then_inc(hid_out[0], 1)
        turn(0)
        with act.Fori(1, NI) as it:
            turn(it)
        layer_norm_act(act, 2)

    def layer_norm(dve, use, src):
        done = [use * LN_STEPS]

        def step(ins):
            done[0] += 1
            ins.then_inc(ln_step, 1)
            dve.wait_ge(ln_step, done[0])

        step(dve.reduce_sum(ln[:, 0, :], src[:, :, :], AX.X))
        step(dve.tensor_scalar(ln[:, 1, :], ln[:, 0, :], 1.0 / D, None, ALU.mult))
        step(dve.tensor_tensor(xn[:, :, :], src[:, :, :], ln[:, 1, :].unsqueeze(2).to_broadcast([P, NT, D]), ALU.subtract))
        dve.wait_ge(ln_sq, use + 1)
        step(dve.reduce_sum(ln[:, 0, :], sq[:, :, :], AX.X))
        step(dve.tensor_scalar(ln[:, 2, :], ln[:, 0, :], 1.0 / D, EPS, ALU.mult, ALU.add))
        dve.wait_ge(ln_sqrt, use + 1)
        step(dve.reciprocal(ln[:, 4, :], ln[:, 3, :]))
        step(dve.tensor_tensor(ln[:, 5, :], ln[:, 4, :], ln[:, 4, :], ALU.mult))
        step(dve.tensor_tensor(ln[:, 5, :], ln[:, 5, :], ln[:, 2, :], ALU.mult))
        step(dve.tensor_scalar(ln[:, 6, :], ln[:, 5, :], -0.5, 1.5, ALU.mult, ALU.add))
        step(dve.tensor_tensor(ln[:, 7, :], ln[:, 4, :], ln[:, 6, :], ALU.mult))

    def vector(dve):
        dve.wait_ge(c_in, C_IN)
        dve.wait_ge(idx_in, 16)
        dve.tensor_copy(idxf[:, :], idx[:, :]).then_inc(top_done, 1)
        dve.wait_ge(top_done, 1)
        for i in range(2):
            dve.tensor_scalar(hot[i][:, :], idxf[:, :], iota[:, i:i + 1], None, ALU.is_equal).then_inc(hot_ready, 1)
        dve.wait_ge(h_in, 16)
        layer_norm(dve, 0, h)
        dve.wait_ge(bias_in, 32)

        def step(t, par, on):
            a, b, c = on
            p1 = 1 - par
            if c:
                dve.wait_ge(exp_done, t - 1)
                dve.reduce_sum(sm[par][:, :], sc[par][:, :, :], AX.X).then_inc(sum_done, 1)
                dve.wait_ge(sum_done, t - 1)
                dve.reciprocal(rs[par][:, :], sm[par][:, :]).then_inc(rs_done, 1)
            if b:
                dve.wait_ge(s_done, t)
                if not isinstance(t, int) or t >= 3:
                    dve.wait_ge(pt_done, t - 2)
                dve.scalar_tensor_tensor(sc[p1][:, :, :].rearrange("p h m -> p (h m)"), bank[3][:, :], HD ** -0.5,
                                         bias[:, :, :].rearrange("p h m -> p (h m)"), ALU.mult, ALU.add).then_inc(s_out, 1)
                dve.wait_ge(s_out, t)
                dve.reduce_max(mx[p1][:, :], sc[p1][:, :, :], AX.X).then_inc(mx_done, 1)
            if a:
                dve.wait_ge(v_done, t + 1)
                reuse(dve, av_done, 1, t)
                dve.tensor_tensor(vd[par][:, :, :].rearrange("p i n -> p (i n)"), bank[2][:, 0:P], v_mask[:, :], ALU.mult)\
                   .then_inc(v_out, 1)
            if c:
                dve.wait_ge(av_done, t - 1)
                dve.wait_ge(rs_done, t - 1)
                reuse(dve, ot_done, 1, t - 2)
                dve.tensor_tensor(o[par][:, :].rearrange("p (h d) -> p h d", h=H), bank[5][:, 0:D].rearrange("p (h d) -> p h d", h=H),
                                  rs[par][:, :].unsqueeze(2).to_broadcast([P, H, HD]), ALU.mult).then_inc(o_out, 1)
                dve.wait_ge(pr_done, t - 1)
                ht_ = tile(h, t - 2)
                dve.tensor_tensor(ht_, bank[7][:, 0:D], ht_, ALU.add).then_inc(pr_out, 1)
        three_stages(dve, step)

        dve.wait_ge(pr_out, NT)
        layer_norm(dve, 1, h)
        dve.tensor_tensor(xn[:, :, :], xn[:, :, :], ln[:, 7, :].unsqueeze(2).to_broadcast([P, NT, D]), ALU.mult).then_inc(x_ready, 1)
        for n in range(NT // 8):
            dve.wait_ge(lg_done, n + 1)
            dve.tensor_copy(lg[:, 8 * n:8 * n + 8, :].rearrange("p t e -> p (t e)"), bank[2 + n % 2][:, 0:8 * NE]).then_inc(lg_out, 1)
        dve.wait_ge(lg_out, NT // 8)
        for t in range(NT):
            dve.max(top[:, t, :], lg[:, t, :]).then_inc(top_done, 1)
        dve.wait_ge(top_done, NT + 1)
        for t in range(NT):
            dve.max_index(topi[:, t, :], top[:, t, :], lg[:, t, :]).then_inc(top_done, 1)

        dve.tensor_tensor(gv[:, 0, :], top[:, :, 1], top[:, :, 0], ALU.subtract).then_inc(gap_ready, 1)
        dve.wait_ge(top_done, 2 * NT + 1)
        done = [0]

        def gstep(ins):
            done[0] += 1
            ins.then_inc(gate_step, 1)
            dve.wait_ge(gate_step, done[0])

        full = [P, NT, NE]
        gstep(dve.tensor_copy(gv[:, 4:6, :].rearrange("p i t -> p t i"), topi[:, :, 0:2]))
        dve.wait_ge(gap_exp, 1)
        gstep(dve.tensor_scalar(gv[:, 2, :], gv[:, 1, :], 1.0, None, ALU.add))
        gstep(dve.reciprocal(gv[:, 2, :], gv[:, 2, :]))
        gstep(dve.tensor_tensor(gv[:, 3, :], gv[:, 2, :], gv[:, 1, :], ALU.mult))
        er = erow[:, :].unsqueeze(1).to_broadcast(full)
        dve.tensor_tensor(gate[:, :, :], er, gv[:, 4, :].unsqueeze(2).to_broadcast(full), ALU.is_equal)
        gstep(dve.tensor_tensor(gate2[:, :, :], er, gv[:, 5, :].unsqueeze(2).to_broadcast(full), ALU.is_equal))
        gstep(dve.tensor_tensor(gate[:, :, :], gate[:, :, :], gv[:, 2, :].unsqueeze(2).to_broadcast(full), ALU.mult))
        gstep(dve.tensor_tensor(gate2[:, :, :], gate2[:, :, :], gv[:, 3, :].unsqueeze(2).to_broadcast(full), ALU.mult))
        gstep(dve.tensor_tensor(gate[:, :, :], gate[:, :, :], gate2[:, :, :], ALU.add))
        assert done[0] == GATE_STEPS
        for n in range(NT // 8):
            dve.wait_ge(gt_done, n + 1)
            dve.tensor_copy(gT[:, n, :], bank[4 + n % 2][:, 0:P]).then_inc(gt_out, 1)
            dve.wait_ge(b2_done, n + 1)
            part = xn[:, 8 * n:8 * n + 8, :].rearrange("p t y -> p (t y)")
            dve.tensor_tensor(part, bank[6 + n % 2][:, :], part, ALU.add).then_inc(b2_out, 1)

        def turn(it):
            now = not isinstance(it, int)

            def gated(half):
                for q in range(2):
                    if now and half == 0:
                        dve.wait_ge(moe_sum, it * 2 - 1 + q)
                    dve.wait_ge(hid_used, it * HJ + 4 * half + 4)
                    dve.tensor_tensor(wo[q][:, half, :].rearrange("p (e y) -> p e y", y=D),
                                      bank[4 + 2 * half + q][:, :].rearrange("p (e y) -> p e y", y=D),
                                      gate[:, bass.ds(it * 2 + q, 1), half * EH:(half + 1) * EH]
                                      .rearrange("p t e -> p (t e)").unsqueeze(2).to_broadcast([P, EH, D]),
                                      ALU.mult).then_inc(eo_out, 1)

            for j in range(1, HJ, 2):
                dve.wait_ge(hid_done, it * HJ + j + 1)
                if now or j >= 4:
                    dve.wait_ge(hid_used, it * HJ + j - 3)
                dve.tensor_scalar(hid[j % 4][:, :, :].rearrange("p i n -> p (i n)"), bank[j % 4][:, :], 0.0, None, ALU.max)\
                   .then_inc(hid_out[1], 1)
                if j == 5:
                    gated(0)
            gated(1)
        turn(0)
        with dve.Fori(1, NI) as it:
            turn(it)

        dve.wait_ge(moe_sum, NT)
        fdone = [0]

        def fstep(ins):
            fdone[0] += 1
            ins.then_inc(fin_step, 1)
            dve.wait_ge(fin_step, fdone[0])

        fstep(dve.tensor_tensor(xn[:, :, :], xn[:, :, :], sq[:, :, :], ALU.add))
        layer_norm(dve, 2, xn)
        big = [P, NT, D]
        fstep(dve.tensor_tensor(xn[:, :, :], xn[:, :, :], ln[:, 7, :].unsqueeze(2).to_broadcast(big), ALU.mult))
        fstep(dve.tensor_tensor(xn[:, :, :], xn[:, :, :], gamma[:, :].unsqueeze(1).to_broadcast(big), ALU.mult))
        fstep(dve.tensor_tensor(xn[:, :, :], xn[:, :, :], beta[:, :].unsqueeze(1).to_broadcast(big), ALU.add))
        fstep(dve.tensor_tensor(h[:, :, :], h[:, :, :], xn[:, :, :], ALU.add))
        assert fdone[0] == FIN_STEPS + 1

    return sync, gpsimd, tensor, scalar, vector


def transforms():
    y = np.arange(S)
    ky = np.arange(M2)
    kx = np.concatenate([np.arange(M1), np.arange(S - M1, S)])
    ay = 2 * np.pi * np.outer(y, ky) / S
    ax = 2 * np.pi * np.outer(y, kx) / S
    col = np.stack([np.cos(ay), -np.sin(ay)], -1)
    fwd_y = np.zeros((2, S, 2, M2, 2))
    for h in range(2):
        fwd_y[h, :, h] = col
    fwd_x = np.zeros((S, 2, KX, 2))
    fwd_x[:, 0, :, 0], fwd_x[:, 0, :, 1] = np.cos(ax), -np.sin(ax)
    fwd_x[:, 1, :, 0], fwd_x[:, 1, :, 1] = np.sin(ax), np.cos(ax)
    inv_x = np.zeros((KX, 2, S, 2))
    inv_x[:, 0, :, 0], inv_x[:, 0, :, 1] = np.cos(ax).T, np.sin(ax).T
    inv_x[:, 1, :, 0], inv_x[:, 1, :, 1] = -np.sin(ax).T, np.cos(ax).T
    weight = np.where(ky == 0, 1.0, 2.0) / (PX // 64)
    back = np.stack([np.cos(ay) * weight, -np.sin(ay) * weight], 1)
    inv_y = np.zeros((4, M2, 2, 4, S))
    for q in range(4):
        inv_y[q, :, :, q, :] = back.transpose(2, 1, 0)
    line = np.linspace(0.0, 1.0, S, dtype=np.float32)
    grid = np.stack([np.repeat(line, S), np.tile(line, S), np.ones(PX, np.float32)])
    full = np.fft.fft2(grid.reshape(3, S, S).astype(np.float64))[:, kx][:, :, ky]
    parts = np.stack([full.real, full.imag], -1).reshape(3, KX, KYH, KY4, 2)
    gspec = parts.transpose(0, 3, 2, 1, 4).reshape(3 * KY4, SPEC)
    f = lambda a, *shape: np.ascontiguousarray(a.reshape(shape), np.float32)

    def split(a, rows, cols):
        a = a.reshape(rows, cols)
        hi = a.astype(np.float16)
        return np.stack([hi, (a - hi).astype(np.float16)], 1)
    return dict(fwd_y=split(fwd_y / 8, P, 48), fwd_x=split(fwd_x / 8, P, 48), inv_x=np.tile(split(inv_x, 48, P), (2, 1, 1)), inv_y=f(inv_y, 96, 256),
                grid=grid, gspec=f(np.tile(gspec / 64, (1, F0B)), 12, FQ))


def kernel(**inputs):
    import concourse.bacc as bacc
    from concourse.bass_utils import run_bass_kernel_spmd

    a = {n.replace("L0_", ""): np.asarray(t) for n, t in inputs.items()}
    eye = np.eye(P, dtype=np.float32)
    same = np.kron(np.ones((GI, GI), np.float32), np.eye(C, dtype=np.float32))
    arrays = dict(transforms(), x=a["x"].reshape(NG, GI, PX), ident=eye, ident16=eye.astype(np.float16), avg=same / GI,
                  quarter=np.full((P, P), 1 / GI, np.float32))

    fw = np.concatenate([a["tok_fw1"], a["tok_fw2"]], axis=3)
    fw = fw.reshape(L, C, C, KX, KYH, KY4, 2).transpose(0, 4, 3, 5, 1, 6, 2)
    fw = fw.reshape(L * NCH, CH, P, 2 * C).transpose(0, 2, 1, 3)
    arrays["fw"] = np.ascontiguousarray(fw).reshape(L * NCH, P, CH * 2 * C)
    wmix = np.zeros((GI, C, L, GI, C), np.float32)
    p16 = np.zeros((4, KY4, KY4, C), np.float32)
    pt7 = np.zeros((GI, C, 7), np.float32)
    qbd = np.zeros((GI, C, GI + 1), np.float32)
    lift = [a["tok_p_w"][0], a["tok_p_w"][1], a["tok_p_w"][2], a["tok_p_b"]]
    for j in range(GI):
        wmix[j, :, :, j, :] = a["tok_w_w"].transpose(1, 0, 2)
        pt7[j, :, j] = lift[0]
        for f in range(4):
            p16[f, j, j] = lift[f]
        for f in range(3):
            pt7[j, :, 4 + f] = lift[1 + f]
        qbd[j, :, j] = a["tok_q_w"][:, 0]
        qbd[j, :, GI] = a["tok_q_w"][:, 0]
    chan = np.stack([a["tok_w_b"].T, a["tok_bn_g"].T, a["tok_bn_b"].T], -1)
    arrays.update(wmix=wmix.reshape(P, L, P), p16=p16.reshape(16, P), pt7=pt7.reshape(P, 7), qbd=qbd.reshape(P, GI + 1),
                  chan=np.tile(chan, (GI, 1, 1)), qb=np.tile(a["tok_q_b"].reshape(1, 1), (P, 1)))

    w_qkv = a["attn_w_qkv"].reshape(3, S, S)
    wqk = np.stack([np.stack([w_qkv[i].T] * 2, 1) for i in range(2)], 1)
    tokens = np.arange(P)
    heads = np.repeat(np.arange(H), HD)
    parity = (tokens[:, None] // S == np.tile(heads, 2)[None, :] % 2)
    arrays.update(
        att_ident=eye, att_wqk=wqk.reshape(S, 4 * S), att_wv=w_qkv[2].T,
        att_wp=np.concatenate([a["attn_w_proj"].T, a["attn_b_proj"][None, :]]),
        att_head_mask=(np.tile(heads, 2)[:, None] == np.arange(H)).astype(np.float32), att_v_mask=parity.astype(np.float32),
        att_iota=np.stack([tokens, tokens + P], 1).astype(np.float32), att_table=a["attn_rel_table"],
        att_index=a["attn_rel_index"].reshape(1, NIDX))
    b2 = np.zeros((8, NE, 8, D), np.float32)
    for i in range(8):
        b2[i, :, i, :] = a["ffn_b2"]
    arrays.update(
        moe_gw=np.concatenate([a["ffn_gate_w"], a["ffn_gate_b"][None, :]]),
        moe_w1=np.concatenate([a["ffn_w1"].transpose(1, 0, 2), a["ffn_b1"][None]]).reshape(D + 1, NE * FF),
        moe_w2=a["ffn_w2"].transpose(1, 0, 2).reshape(FF, NE * D), moe_b2=b2.reshape(P, 8 * D),
        moe_gamma=np.tile(a["ffn_gamma"][None, :], (P, 1)), moe_beta=np.tile(a["ffn_beta"][None, :], (P, 1)),
        moe_erow=np.tile(np.arange(NE, dtype=np.float32)[None, :], (P, 1)))

    nc = bacc.Bacc("TRN2", target_bir_lowering=False, num_devices=1)
    arrays = {n: np.ascontiguousarray(t) for n, t in arrays.items()}
    d = {n: nc.dram_tensor(n, t.shape, mybir.dt.from_np(t.dtype), kind="ExternalInput").ap() for n, t in arrays.items()}
    att = {n[4:]: d.pop(n) for n in list(d) if n.startswith("att_")}
    moe = {n[4:]: d.pop(n) for n in list(d) if n.startswith("moe_")}
    out = nc.dram_tensor("out", (B, S, S), F32, kind="ExternalOutput").ap()
    build(nc, out=out, att=att, moe=moe, **d)
    r = run_bass_kernel_spmd(nc, [arrays], core_ids=[0])
    return r.results[0]["out"]
```

```python
from contextlib import ExitStack

import numpy as np

import concourse.bass as bass
from concourse import mybir

F32 = mybir.dt.float32
F16 = mybir.dt.float16
I32 = mybir.dt.int32
U32 = mybir.dt.uint32
ALU = mybir.AluOpType
ACT = mybir.ActivationFunctionType
AX = mybir.AxisListType

B, S, C, L = 128, 64, 32, 4
PX = S * S
M1 = M2 = 12
KX, KYH, KY4 = 2 * M1, M2 // 4, 4
P = 128
GI = P // C
NG = B // GI
HG = NG // 2
MODES = KYH * KX
SPEC = MODES * 2
CH = 6
NCH = MODES // CH
MJ = CH // 2
MIX_BANKS = 2 * MJ
TJ, YJ, T2J, XJ = 8, 4, 3, 2
T3J, XIJ, T4J, FJ = 3, 3, 4, 8
F0B = 16
F0J = 6
NF0 = B // F0B
FQ = F0B * SPEC
X7_ROWS = (0, 32, 64)
X7_LOADS = 16 * len(X7_ROWS)
EPS = 1e-5
BN_STEPS = 13


def pipelined(eng, step, fresh=False):
    step(0, 0, 0, True, False)
    if fresh:
        step(1, 0, 1, True, True)
        step(2, 1, 0, True, True)
    with eng.Fori(1 if fresh else 0, HG - 1) as i:
        step(i * 2 + 1, i, 1, True, True)
        step(i * 2 + 2, i + 1, 0, True, True)
    step(NG - 1, HG - 1, 1, True, True)
    step(NG, HG, 0, False, True)


def half_before(h, par):
    return h if par else h - 1


def by_pairs(eng, layer, count, step):
    if isinstance(layer, int):
        step(0, 0, 0)
        step(1, 0, 1)
    with eng.Fori(1 if isinstance(layer, int) else 0, count // 2) as i:
        step(i * 2, i, 0)
        step(i * 2 + 1, i, 1)


INVERSE = (("t3", 0), ("t3", 1), ("final", 0), ("t3", 2), ("final", 1), ("final", 2), ("xi", 0), ("xi", 1), ("final", 3),
           ("xi", 2), ("final", 4), ("t4", 0), ("t4", 1), ("final", 5), ("t4", 2), ("final", 6), ("t4", 3), ("final", 7))


def inverse_order(head, tail, **jobs):
    for name, i in INVERSE:
        if name in jobs and (tail if name == "final" else head):
            jobs[name](i)


def reuse(eng, done, per, n):
    if not isinstance(n, int):
        eng.wait_ge(done, (n - 1) * per)
    elif n >= 2:
        eng.wait_ge(done, (n - 1) * per)


def bank_free(eng, emptied, job, ring=2):
    if not isinstance(job, int) or job >= ring:
        eng.wait_ge(emptied, job - (ring - 1))


def forward_use(l):
    return l * (2 * NG) - NG


def inverse_use(l):
    return l * (2 * NG)


FINAL_USE = L * 2 * NG - NG


def build(nc, x, fw, wmix, chan, p16, pt7, grid, gspec, fwd_y, fwd_x, inv_x, inv_y, ident, ident16, avg, quarter,
          qbd, qb, att, moe, out):
    u_dram = nc.dram_tensor("u_pixels", [NG, P, PX], F32, kind="Internal").ap()
    fx_dram = nc.dram_tensor("x_spectrum", [B, KYH, KY4, 2 * KX], F32, kind="Internal").ap()
    h_dram = nc.dram_tensor("h_tokens", [NG, GI, PX], F32, kind="Internal").ap()

    with ExitStack() as ctx:
        def sem(name):
            return ctx.enter_context(nc.semaphore(name))

        def pair(name):
            return [sem(f"{name}{s}") for s in range(2)]

        bank = [ctx.enter_context(nc.psum_tensor(f"bank{i}", [P, 512], F32)) for i in range(8)]

        fno = ExitStack()

        def sb(name, shape, dt=F32):
            return fno.enter_context(nc.sbuf_tensor(name, shape, dt))

        spec = sb("spec", [P, B, SPEC])
        v = [sb(f"v{s}", [P, PX]) for s in range(2)]
        pix = [sb(f"pix{s}", [P, PX]) for s in range(2)]
        rowf = [sb(f"rowf{s}", [P, 2 * M2 * S]) for s in range(2)]
        rowt = [sb(f"rowt{s}", [P, 2 * M2 * S]) for s in range(2)]
        wide = sb("wide", [P, 2 * CH * 3 * P])
        og = [sb(f"og{s}", [P, GI * SPEC]) for s in range(2)]
        wd = [sb(f"wd{s}", [P, CH * 2 * C]) for s in range(2)]
        stats = sb("stats", [P, NG * FJ * 6])
        wm = sb("wm", [P, L, P])
        wcur = sb("wcur", [P, P])
        wx7 = sb("wx7", [96, P], F16)
        x7 = sb("x7", [96, PX], F16)
        pt7_sb = sb("pt7_sb", [P, 96])
        p16_sb = sb("p16_sb", [16, P])
        fy = sb("fy", [P, 2, 48], F16)
        fx = sb("fx", [P, 2, 48], F16)
        ix = sb("ix", [96, 2, P], F16)
        idn16 = sb("idn16", [P, P], F16)
        iy = sb("iy", [96, 2, P], F16)
        idn = sb("idn", [P, P])
        avg_sb = sb("avg_sb", [P, P])
        quarter_sb = sb("quarter_sb", [P, P])
        chan_sb = sb("chan_sb", [P, L, 3])
        qbd_sb = sb("qbd_sb", [P, GI + 1])
        qcol = sb("qcol", [P, GI])
        qb_sb = sb("qb_sb", [P, 1])
        bn = sb("bn", [P, 32])
        fno.close()

        HALF = CH * 3 * P
        bd = [wide[:, s * HALF:(s + 1) * HALF].rearrange("p (m t n) -> p m t n", m=CH, t=3) for s in range(2)]
        ht = [wide[0:96, s * 2048:(s + 1) * 2048].bitcast(F16).rearrange("p (q n) -> p q n", n=P) for s in range(2)]
        f0_rows = [wide[0:16, s * FQ:(s + 1) * FQ] for s in range(2)]
        spec_flat = spec[:, :, :].rearrange("p b s -> p (b s)")

        def halves(t):
            n = t.shape[1] // 2
            return t[:, 0:n].bitcast(F16), t[:, n:2 * n].bitcast(F16)

        pix_hi, pix_lo = zip(*[halves(t) for t in pix])
        rowt_hi, rowt_lo = zip(*[halves(t) for t in rowt])
        og16 = [t[:, :].bitcast(F16).rearrange("p (n t m) -> p n t m", t=2, m=2 * KX) for t in og]
        xrows = [t[:, :].bitcast(F16).rearrange("p (x t k r) -> p t k x r", t=2, k=M2, r=2) for t in rowf]
        xrows_flat = [t[:, :].bitcast(F16) for t in rowf]
        kxt = [t[0:96, 0:M2 * P // 2].bitcast(F16) for t in rowt]
        wds = [t[:, :].rearrange("p (m r o) -> p m r o", m=CH, r=2) for t in wd]
        bias_l = bn[:, 16:17]
        scale_l = bn[:, 17:18]
        gamma, beta, wb = bn[:, 18:19], bn[:, 19:20], bn[:, 20:21]
        hconst = bn[:, 21:22]

        waited = sem("waited")
        const_in, x_in, f0_const_in, fx_out = sem("const_in"), sem("x_in"), sem("f0_const_in"), sem("fx_out")
        f0_in, v_in, x7_in, wd_in = pair("f0_in"), pair("v_in"), pair("x7_in"), pair("wd_in")
        vf_in = [pair(f"vf_in{half}") for half in range(2)]
        v_first = sem("v_first")
        v_used, relu_done = sem("v_used"), sem("relu_done")
        t_done, t_hi, t_out = sem("t_done"), sem("t_hi"), sem("t_out")
        y_done, y_out = sem("y_done"), sem("y_out")
        t2_done, t2_hi, t2_out = sem("t2_done"), sem("t2_hi"), sem("t2_out")
        x_done, x_out = sem("x_done"), sem("x_out")
        f0_done, f0_out = sem("f0_done"), pair("f0_out")
        bd_zero, bd_ready = sem("bd_zero"), sem("bd_ready")
        mix_done, mix_out = sem("mix_done"), sem("mix_out")
        og_hi, og_ready = sem("og_hi"), sem("og_ready")
        t3_done, t3_out = sem("t3_done"), sem("t3_out")
        xi_done, xi_hi, xi_out = sem("xi_done"), sem("xi_hi"), sem("xi_out")
        t4_done, t4_out = sem("t4_done"), sem("t4_out")
        fin_done, fin_out = sem("fin_done"), sem("fin_out")
        stats_done = sem("stats_done")
        u_stored = pair("u_stored")
        v_zero, x7_hi, x7_split, w7_hi = sem("v_zero"), sem("x7_hi"), sem("x7_split"), sem("w7_hi")
        w_ready, w7_done, w7_ready = sem("w_ready"), sem("w7_done"), sem("w7_ready")
        bn_step, bn_avg, bn_sqrt = sem("bn_step"), sem("bn_avg"), sem("bn_sqrt")
        q_step, q_sum, q_ready = sem("q_step"), sem("q_sum"), sem("q_ready")
        head_done, head_out = sem("head_done"), pair("head_out")
        h_stored = pair("h_stored")

        consts = ((fy, fwd_y), (fx, fwd_x), (ix, inv_x), (iy, inv_y), (idn, ident), (idn16, ident16), (avg_sb, avg),
                  (quarter_sb, quarter), (wm, wmix), (chan_sb, chan), (p16_sb, p16), (pt7_sb, pt7),
                  (qbd_sb, qbd), (qb_sb, qb))
        CONST = 16 * len(consts)

        tok_sync, tok_gpsimd, tok_tensor, tok_scalar, tok_vector = token_programs(
            nc, ctx, bank, sem, h_dram, h_stored, att, moe, out)
        block = ctx.enter_context(nc.Block())

        def alone(eng):
            eng.sem_inc(waited, 1)

        @block.sync
        def _(sp):
            for dst, src in consts:
                sp.dma_start(dst[:], src).then_inc(const_in, 16)
            sp.dma_start(v[0][:, :], x.rearrange("g i n -> (g i) n")).then_inc(x_in, 16)
            for s in range(2):
                sp.dma_start(f0_rows[s][4:16, :], gspec).then_inc(f0_const_in, 16)
                sp.dma_start(wd[s][:, :], fw[s]).then_inc(wd_in[s], 16)
            sp.wait_ge(x_out, XJ)
            sp.dma_start(fx_dram.rearrange("b h k m -> b (h k m)"), og[0][:, :]).then_inc(fx_out, 16)
            sp.wait_ge(fx_out, 16)
            for q in range(NF0):
                if q >= 2:
                    sp.wait_ge(f0_done, F0J * (q - 1))
                for k4 in range(KY4):
                    sp.dma_start(f0_rows[q % 2][k4:k4 + 1, :].rearrange("k (b h m) -> k b h m", b=F0B, h=KYH),
                                 fx_dram[q * F0B:(q + 1) * F0B, :, k4:k4 + 1, :].rearrange("b h k m -> k b h m"))\
                      .then_inc(f0_in[q % 2], 16)

            def load_weights(first):
                with sp.Fori(1, NCH // 2) as i:
                    for par in range(2):
                        sp.wait_ge(bd_ready, first + i * 2 + par - 1)
                        sp.dma_start(wd[par][:, :], fw[first + i * 2 + par]).then_inc(wd_in[par], 16)

            def store(l, g, par):
                sp.wait_ge(fin_out, (l * NG + g) * FJ + FJ)
                sp.dma_start(u_dram[g], pix[par][:, :]).then_inc(u_stored[par], 16)

            load_weights(0)
            def load_x(g, par):
                for at in X7_ROWS:
                    sp.dma_start(v[par][at:at + GI, :], x[g]).then_inc(x7_in[par], 16)

            sp.wait_ge(v_zero, 2)
            for s in range(2):
                for at in X7_ROWS:
                    sp.dma_start(v[s][at + GI:at + GI + 3, :], grid).then_inc(x7_in[s], 16)
                load_x(s, s)
            with sp.Fori(0, HG - 1) as i:
                for par in range(2):
                    g = i * 2 + par
                    sp.wait_ge(v_used, g + 1)
                    load_x(g + 2, par)
                    store(0, g, par)
            for g in (NG - 2, NG - 1):
                store(0, g, g % 2)

            with sp.Fori(1, L) as l:
                for par in range(2):
                    sp.wait_ge(bd_ready, l * NCH + par - 1)
                    sp.dma_start(wd[par][:, :], fw[l * NCH + par]).then_inc(wd_in[par], 16)
                def load_half(g, par, half):
                    px = slice(half * (PX // 2), (half + 1) * (PX // 2))
                    sp.dma_start(v[par][:, px], u_dram[g][:, px]).then_inc(vf_in[half][par], 16)

                for par in range(2):
                    sp.wait_ge(v_used, forward_use(l) + par - 1)
                    sp.wait_ge(u_stored[par], ((l - 1) * HG + 1) * 16)
                    load_half(par, par, 0)
                    load_half(par, par, 1)
                with sp.Fori(1, HG) as i:
                    for par in range(2):
                        sp.wait_ge(v_first, (l - 1) * NG + i * 2 + par - 1)
                        sp.wait_ge(u_stored[par], ((l - 1) * HG + i + 1) * 16)
                        load_half(i * 2 + par, par, 0)
                        sp.wait_ge(v_used, forward_use(l) + i * 2 + par - 1)
                        load_half(i * 2 + par, par, 1)
                load_weights(l * NCH)
                for par in range(2):
                    sp.wait_ge(v_used, inverse_use(l) + par - 1)
                    sp.dma_start(v[par][:, :], u_dram[par]).then_inc(v_in[par], 16)
                with sp.Fori(0, HG - 1) as i:
                    for par in range(2):
                        g = i * 2 + par
                        sp.wait_ge(v_used, inverse_use(l) + g + 1)
                        sp.dma_start(v[par][:, :], u_dram[g + 2]).then_inc(v_in[par], 16)
                        store(l, g, par)
                for g in (NG - 2, NG - 1):
                    store(l, g, g % 2)

            def load_last(i, par):
                if isinstance(i, int):
                    sp.wait_ge(v_used, FINAL_USE + par - 1)
                else:
                    sp.wait_ge(head_done, (i * 2 + par - 1) * FJ)
                sp.wait_ge(u_stored[par], ((L - 1) * HG + i + 1) * 16)
                sp.dma_start(v[par][:, :], u_dram[i * 2 + par]).then_inc(v_in[par], 16)

            def store_h(g, par):
                for s in range(2):
                    sp.wait_ge(head_out[s], (g + 1) * (FJ // 2))
                sp.dma_start(h_dram[g], pix[par][0:GI, :]).then_inc(h_stored[par], 16)

            for par in range(2):
                load_last(0, par)
            with sp.Fori(0, HG - 1) as i:
                for par in range(2):
                    load_last(i + 1, par)
                    store_h(i * 2 + par, par)
            for g in (NG - 2, NG - 1):
                store_h(g, g % 2)
            tok_sync(sp)

        @block.gpsimd
        def _(gp):
            def clear(l):
                if isinstance(l, int):
                    gp.wait_ge(f0_done, NF0 * F0J)
                else:
                    gp.wait_ge(fin_done, l * (NG * FJ))
                alone(gp)
                gp.memset(wide[:, :], 0.0).then_inc(bd_zero, 1)

            def take(l):
                gp.wait_ge(mix_out, (l + 1) * (NCH * MJ))
                alone(gp)

                first = isinstance(l, int)

                def x_lo(g, par, copied):
                    for i in range(4):
                        gp.wait_ge(x7_hi, g * 4 + i + 1)
                        if i == 0:
                            gp.wait_ge(og_ready, copied)
                        alone(gp)
                        px = slice(i * 1024, (i + 1) * 1024)
                        gp.tensor_tensor(x7[32:64, px], v[par][32:64, px], x7[32:64, px], ALU.subtract).then_inc(x7_split, 1)

                def step(g, h, par):
                    if first and (not isinstance(g, int) or g >= 2):
                        gp.wait_ge(x7_split, (g - 1) * 4)
                    reuse(gp, t3_done, T3J, l * NG + g)
                    src = spec_flat[:, bass.ds(g * (GI * SPEC), GI * SPEC)].rearrange("p (n m) -> p n m", m=2 * KX)
                    gp.tensor_copy(og16[par][:, :, 0, :], src).then_inc(og_hi, 1)
                    gp.wait_ge(og_hi, l * NG + g + 1)
                    alone(gp)
                    gp.tensor_tensor(og16[par][:, :, 1, :], src, og16[par][:, :, 0, :], ALU.subtract).then_inc(og_ready, 1)
                    if first and (not isinstance(g, int) or g >= 1):
                        x_lo(g - 1, 1 - par, g + 1)
                by_pairs(gp, l, NG, step)
                if first:
                    x_lo(NG - 1, (NG - 1) % 2, NG)

            gp.wait_ge(t_done, TJ)
            for t in v:
                gp.memset(t[0:96, :], 0.0).then_inc(v_zero, 1)
            clear(0)
            take(0)
            with gp.Fori(1, L) as l:
                clear(l)
                take(l)
            tok_gpsimd(gp)

        @block.tensor
        def _(pe):
            def transposes(src, i):
                out = bank[i % 2][:, :].rearrange("p (x n) -> p x n", n=P)
                for q in range(4):
                    mm = pe.transpose(out[:, q, :], src[:, (4 * i + q) * P:(4 * i + q + 1) * P], idn[:, :])
                return mm

            def split_product(out, hi, lo, w):
                pe.matmul(out, hi, w[:, 0, :], start=True, stop=False)
                pe.matmul(out, hi, w[:, 1, :], start=False, stop=False)
                return pe.matmul(out, lo, w[:, 0, :], start=False, stop=True)

            def forward_y(par, i, used=None):
                out = bank[2 + i % 2][:, 0:8 * 48].rearrange("p (x m) -> p x m", m=48)
                for q in range(8):
                    x2 = slice((8 * i + q) * P, (8 * i + q + 1) * P)
                    mm = split_product(out[:, q, :], pix_hi[par][:, x2], pix_lo[par][:, x2], fy)
                    if q == 0 and used is not None:
                        mm.then_inc(used, 1)
                mm.then_inc(y_done, 1)

            def forward_rows(par, i, flip):
                out = bank[4 + (flip + par + i) % 2][:, :].rearrange("p (k n) -> p k n", n=P)
                for q in range(4):
                    k = 4 * i + q
                    mm = pe.transpose(out[:, q, :], rowf[par][:, k * P:(k + 1) * P], idn[:, :])
                mm.then_inc(t2_done, 1)

            def forward_x(par, i):
                out = bank[6 + i][:, 0:6 * 48].rearrange("p (n m) -> p n m", m=48)
                for q in range(6):
                    n = 6 * i + q
                    b = slice(n * P, (n + 1) * P)
                    mm = split_product(out[:, q, :], rowt_hi[par][:, b], rowt_lo[par][:, b], fx)
                mm.then_inc(x_done, 1)

            def first_forward():
                pe.wait_ge(const_in, CONST)
                pe.wait_ge(x_in, 16)
                for i in range(TJ):
                    bank_free(pe, t_out, i)
                    transposes(v[0], i).then_inc(t_done, 1)
                for i in range(YJ):
                    pe.wait_ge(t_out, 2 * i + 2)
                    bank_free(pe, y_out, i)
                    forward_y(0, i)
                for i in range(T2J):
                    pe.wait_ge(y_out, YJ)
                    bank_free(pe, t2_out, i)
                    forward_rows(0, i, 0)
                for i in range(XJ):
                    pe.wait_ge(t2_out, T2J)
                    forward_x(0, i)
                pe.wait_ge(f0_const_in, 32)
                for q in range(NF0):
                    pe.wait_ge(f0_in[q % 2], 16 * KY4 * (q // 2 + 1))
                    for i in range(F0J):
                        n = q * F0J + i
                        if n >= 2:
                            pe.wait_ge(f0_out[n % 2], n // 2)
                        pe.matmul(bank[4 + n % 2][:, 0:384], p16_sb[:, :],
                                  f0_rows[q % 2][:, i * 384:(i + 1) * 384], start=True, stop=True)\
                          .then_inc(f0_done, 1)
                pe.sem_inc(t2_done, 1)
                pe.sem_inc(x_done, 1)

            def forward(l):
                def step(g, h, par, head, tail_):
                    a = (l - 1) * NG + g
                    k = forward_use(l) + g

                    def t(i):
                        if i % 2 == 0:
                            pe.wait_ge(relu_done, (k - NG) * 4 + i // 2 + 1)
                        bank_free(pe, t_out, (a + 1) * TJ + i)
                        transposes(v[par], i).then_inc(t_done, 1)

                    def y(i):
                        pe.wait_ge(t_out, (a + 1) * TJ + 2 * i + 2)
                        bank_free(pe, y_out, (a + 1) * YJ + i)
                        forward_y(par, i, {0: v_first, 2: v_used}.get(i))

                    def t2(i):
                        pe.wait_ge(y_out, (a - 1 + 1) * YJ + YJ)
                        bank_free(pe, t2_out, a * T2J + i)
                        forward_rows(1 - par, i, 1)

                    def xs(i):
                        pe.wait_ge(t2_out, a * T2J + T2J)
                        bank_free(pe, x_out, a * XJ + i)
                        forward_x(1 - par, i)

                    for i in range(YJ):
                        if head:
                            t(2 * i), t(2 * i + 1)
                        if tail_ and i < T2J:
                            t2(i)
                        if head and i:
                            y(i - 1)
                    if tail_:
                        xs(0)
                    if head:
                        y(3)
                    if tail_:
                        xs(1)
                pipelined(pe, step)

            def mix(l):
                if isinstance(l, int):
                    for s in range(2):
                        pe.wait_ge(f0_out[s], NF0 * F0J // 2)
                else:
                    pe.wait_ge(x_out, (l * NG + 1) * XJ)
                alone(pe)

                def step(c, h, par):
                    m = l * NCH + c
                    pe.wait_ge(bd_ready, m + 1)
                    for i in range(MJ):
                        job = m * MJ + i
                        bank_free(pe, mix_out, job, MIX_BANKS)
                        acc = bank[(par * MJ + i) % MIX_BANKS][:, :].rearrange("p (m r b) -> p m r b", m=2, r=2)
                        for j in range(2):
                            w = bd[par][:, 2 * i + j]
                            at = (c * CH + (2 * i + j)) * 2
                            fr = spec[:, :, bass.ds(at, 1)].rearrange("p b m -> p (b m)")
                            fi = spec[:, :, bass.ds(at + 1, 1)].rearrange("p b m -> p (b m)")
                            pe.matmul(acc[:, j, 0, :], w[:, 0, :], fr, start=True, stop=False)
                            pe.matmul(acc[:, j, 0, :], w[:, 2, :], fi, start=False, stop=True)
                            pe.matmul(acc[:, j, 1, :], w[:, 1, :], fr, start=True, stop=False)
                            mm = pe.matmul(acc[:, j, 1, :], w[:, 0, :], fi, start=False, stop=True)
                        mm.then_inc(mix_done, 1)
                by_pairs(pe, l, NCH, step)

            def inverse(l):
                first = isinstance(l, int)
                pe.wait_ge(w7_ready if first else w_ready, 1 if first else l)

                def step(g, h, par, head, tail_):
                    n = l * NG + g
                    p0 = 1 - par

                    def t3(i):
                        pe.wait_ge(og_ready, n + 1)
                        bank_free(pe, t3_out, n * T3J + i)
                        alone(pe)
                        out = bank[(par + i) % 2][0:96, 0:256].bitcast(F16).rearrange("p (b n) -> p b n", n=P)
                        for j in range(GI):
                            mm = pe.transpose(out[:, j, :], og16[par][:, j * KYH + i].rearrange("p t m -> p (t m)"), idn16[:, :])
                        mm.then_inc(t3_done, 1)

                    def xi(i):
                        pe.wait_ge(t3_out, n * T3J + i + 1)
                        bank_free(pe, xi_out, n * XIJ + i)
                        out = bank[2 + (par + i) % 2][:, :].rearrange("p (k n) -> p k n", n=P)
                        for q in range(4):
                            k = 4 * i + q
                            rows = kxt[par][:, k * P:(k + 1) * P]
                            pe.matmul(out[:, q, :], rows, ix[:, 0, :], start=True, stop=False)
                            mm = pe.matmul(out[:, q, :], rows, ix[:, 1, :], start=False, stop=True)
                        mm.then_inc(xi_done, 1)

                    def t4(i):
                        pe.wait_ge(xi_out, (n + 1) * XIJ)
                        bank_free(pe, t4_out, n * T4J + i)
                        out = bank[4 + i % 2][0:96, :].bitcast(F16).rearrange("p (q n) -> p q n", n=P)
                        for q in range(8):
                            at = (8 * i + q) * 96
                            mm = pe.transpose(out[:, q, :], xrows_flat[par][:, at:at + 96], idn16[:, :])
                        mm.then_inc(t4_done, 1)

                    def final(i):
                        if first:
                            if i % 2 == 0:
                                pe.wait_ge(x7_split, (g - 1) * 4 + i // 2 + 1)
                        elif i % 2 == 0:
                            pe.wait_ge(relu_done, (inverse_use(l) + g - 1 - NG) * 4 + i // 2 + 1)
                        pe.wait_ge(t4_out, (n - 1) * T4J + i // 2 + 1)
                        bank_free(pe, fin_out, (n - 1) * FJ + i)
                        out = bank[6 + i % 2]
                        if first:
                            mm = pe.matmul(out[:, :], wx7[:, :], x7[:, i * 512:(i + 1) * 512], start=True, stop=False)
                        else:
                            mm = pe.matmul(out[:, :], wcur[:, :], v[p0][:, i * 512:(i + 1) * 512], start=True, stop=False)
                        if i == FJ - 1:
                            mm.then_inc(v_used, 1)
                        for q in range(4):
                            for t in range(2):
                                mm = pe.matmul(out[:, q * P:(q + 1) * P], ht[p0][:, 4 * i + q, :], iy[:, t, :],
                                               start=False, stop=(q == 3 and t == 1))
                        mm.then_inc(fin_done, 1)

                    inverse_order(head, tail_, t3=t3, xi=xi, t4=t4, final=final)
                pipelined(pe, step, first)

            def average(l):
                pe.wait_ge(bn_step, l * BN_STEPS + 3)
                pe.matmul(bank[0][:, 0:2], avg_sb[:, :], bn[:, 2:4], start=True, stop=True).then_inc(bn_avg, 1)

            def layer0_weights():
                pe.wait_ge(mix_out, NCH * MJ)
                pe.matmul(bank[2][0:96, 0:P], pt7_sb[:, :], wm[:, 0, :], start=True, stop=True).then_inc(w7_done, 1)

            first_forward()
            mix(0)
            layer0_weights()
            inverse(0)
            average(0)
            with pe.Fori(1, L) as l:
                forward(l)
                mix(l)
                inverse(l)
                average(l)

            pe.wait_ge(q_step, 1)
            pe.matmul(bank[4][:, 0:1], quarter_sb[:, :], bn[:, 22:23], start=True, stop=True).then_inc(q_sum, 1)
            pe.wait_ge(q_ready, 1)

            def step(g, h, par, head, tail_):
                if head:
                    pe.wait_ge(v_in[par], ((L - 1) * HG + h + 1) * 16)
                    for i in range(FJ):
                        if not isinstance(g, int) or g >= 1:
                            pe.wait_ge(head_out[i % 2], g * (FJ // 2) - (FJ // 2 - 1) + i // 2)
                        pe.matmul(bank[i][0:GI, :], qcol[:, :], v[par][:, i * 512:(i + 1) * 512], start=True, stop=True)\
                          .then_inc(head_done, 1)
            pipelined(pe, step, True)
            tok_tensor(pe)

        @block.scalar
        def _(act):
            def first_forward():
                act.wait_ge(const_in, CONST)
                for i in range(TJ):
                    act.wait_ge(t_done, i + 1)
                    rows_hi(0, i)
                for i in range(YJ):
                    act.wait_ge(y_done, i + 1)
                    columns_out(0, i).then_inc(y_out, 1)
                for i in range(XJ):
                    act.wait_ge(x_done, i + 1)
                    act.copy(og[0][:, i * 288:(i + 1) * 288], bank[6 + i][:, 0:288]).then_inc(x_out, 1)
                for n in range(0, NF0 * F0J, 2):
                    act.wait_ge(f0_done, n + 1)
                    act.copy(spec_flat[:, n * 384:(n + 1) * 384], bank[4][:, 0:384]).then_inc(f0_out[0], 1)

            def rows_hi(par, i):
                act.copy(pix_hi[par][:, i * 512:(i + 1) * 512], bank[i % 2][:, :]).then_inc(t_hi, 1)

            def columns_out(par, i):
                dst = rowf[par][:, :].rearrange("p (k x r) -> p x k r", k=M2, r=2)[:, 16 * i:16 * i + 16]
                src = bank[2 + i % 2][:, 0:384].rearrange("p (x k r) -> p x k r", k=M2, r=2)
                return act.copy(dst, src)

            def activate(n, par, quarters=range(4), halves_in=None):
                for i in quarters:
                    if halves_in:
                        act.wait_ge(halves_in[i // 2][par], (n + 1) * 16)
                    else:
                        act.wait_ge(v_in[par], (n + 1) * 16)
                    px = v[par][:, i * 1024:(i + 1) * 1024]
                    act.activation(px, px, ACT.Relu, bias=bias_l, scale=scale_l).then_inc(relu_done, 1)

            def forward(l):
                act.wait_ge(bn_step, l * BN_STEPS)
                for s in range(2):
                    act.wait_ge(u_stored[s], l * HG * 16)
                activate((l - 1) * HG, 0, halves_in=vf_in)

                def step(g, h, par, head, tail_):
                    a = (l - 1) * NG + g

                    def columns(i):
                        act.wait_ge(y_done, (a + 1) * YJ + i + 1)
                        columns_out(par, i).then_inc(y_out, 1)

                    if head:
                        act.wait_ge(y_done, a * YJ + 1)
                        act.wait_ge(t2_done, a * T2J + 1)
                        for i in range(YJ):
                            for j in (2 * i, 2 * i + 1):
                                act.wait_ge(t_done, (a + 1) * TJ + j + 1)
                                rows_hi(par, j)
                            if i >= 2:
                                columns(i - 2)
                            if not isinstance(g, int) or g < NG - 1:
                                activate((l - 1) * HG + h + par, 1 - par, (i,), vf_in)
                        columns(2)
                        columns(3)
                pipelined(act, step)

            def mix(l):
                def step(c, h, par):
                    for i in range(MJ):
                        act.wait_ge(mix_done, (l * NCH + c) * MJ + i + 1)
                        src = bank[(par * MJ + i) % MIX_BANKS][:, :].rearrange("p (m b) -> p m b", b=B)
                        dst = spec[:, :, bass.ds((c * CH + 2 * i) * 2, 4)].rearrange("p b m -> p m b")
                        act.copy(dst, src).then_inc(mix_out, 1)
                by_pairs(act, l, NCH, step)

            def inverse(l):
                first = isinstance(l, int)
                act.wait_ge(w7_ready if first else w_ready, 1 if first else l)

                def step(g, h, par, head, tail_):
                    n = l * NG + g
                    p0 = 1 - par

                    def final(i):
                        act.wait_ge(fin_done, (n - 1) * FJ + i + 1)
                        act.activation(pix[p0][:, i * 512:(i + 1) * 512], bank[6 + i % 2][:, :], ACT.Identity, bias=wb)\
                           .then_inc(fin_out, 1)

                    def final_and_next(i):
                        final(i)
                        if i >= 4:
                            next_pixels(i - 4)

                    def next_pixels(i):
                        if head and not first:
                            activate((l - 1) * HG + h, par, (i,))
                        if head and first:
                            act.wait_ge(x7_in[par], (h + 2) * X7_LOADS)
                            px = slice(i * 1024, (i + 1) * 1024)
                            act.copy(x7[:, px], v[par][0:96, px]).then_inc(x7_hi, 1)

                    def xi(i):
                        act.wait_ge(xi_done, n * XIJ + i + 1)
                        src = bank[2 + (par + i) % 2][:, :].rearrange("p (k x r) -> p k x r", k=4, r=2)
                        act.copy(xrows[par][:, 0, 4 * i:4 * i + 4], src).then_inc(xi_hi, 1)

                    if tail_:
                        if not isinstance(n, int) or n >= 3:
                            act.wait_ge(stats_done, (n - 2) * FJ)
                            act.wait_ge(u_stored[p0], (l * HG + half_before(h, par)) * 16)
                    if head:
                        reuse(act, t4_done, T4J, n)
                    inverse_order(head, tail_, xi=xi, final=final_and_next)
                    if not tail_:
                        for i in range(4):
                            next_pixels(i)
                pipelined(act, step, first)

            def deviation(l):
                act.wait_ge(bn_step, l * BN_STEPS + 6)
                act.activation(bn[:, 9:10], bn[:, 8:9], ACT.Sqrt).then_inc(bn_sqrt, 1)

            first_forward()
            mix(0)
            inverse(0)
            deviation(0)
            with act.Fori(1, L) as l:
                forward(l)
                mix(l)
                inverse(l)
                deviation(l)

            act.wait_ge(q_ready, 1)

            for q in range(2):
                act.wait_ge(u_stored[q], L * HG * 16)

            def step(g, h, par, head, tail_):
                if head:
                    if not isinstance(g, int) or g >= 2:
                        act.wait_ge(h_stored[par], h * 16)
                    for i in range(0, FJ, 2):
                        act.wait_ge(head_done, g * FJ + i + 1)
                        act.activation(pix[par][0:GI, i * 512:(i + 1) * 512], bank[i][0:GI, :], ACT.Identity,
                                       bias=hconst[0:GI, :]).then_inc(head_out[0], 1)
            pipelined(act, step, True)
            tok_scalar(act)

        @block.vector
        def _(dve):
            def rows_lo(par, i):
                px = slice(i * 512, (i + 1) * 512)
                dve.tensor_tensor(pix_lo[par][:, px], bank[i % 2][:, :], pix_hi[par][:, px], ALU.subtract).then_inc(t_out, 1)

            def first_forward():
                dve.wait_ge(const_in, CONST)
                for i in range(TJ):
                    dve.wait_ge(t_hi, i + 1)
                    rows_lo(0, i)
                for i in range(T2J):
                    dve.wait_ge(t2_done, i + 1)
                    b = slice(i * 512, (i + 1) * 512)
                    dve.tensor_copy(rowt_hi[0][:, b], bank[4 + i % 2][:, :]).then_inc(t2_hi, 1)
                    dve.wait_ge(t2_hi, i + 1)
                    dve.tensor_tensor(rowt_lo[0][:, b], bank[4 + i % 2][:, :], rowt_hi[0][:, b], ALU.subtract).then_inc(t2_out, 1)
                for n in range(1, NF0 * F0J, 2):
                    dve.wait_ge(f0_done, n + 1)
                    dve.tensor_copy(spec_flat[:, n * 384:(n + 1) * 384], bank[5][:, 0:384]).then_inc(f0_out[1], 1)

            def forward(l):
                for s in range(2):
                    dve.wait_ge(u_stored[s], l * HG * 16)
                dve.wait_ge(og_ready, l * NG)

                def step(g, h, par, head, tail_):
                    a = (l - 1) * NG + g
                    p0 = 1 - par

                    def t2(i):
                        dve.wait_ge(t2_done, a * T2J + i + 2)
                        hi, lo = (t[p0].rearrange("p (b k c) -> p k b c", k=M2, c=C)[:, 4 * i:4 * i + 4]
                                  for t in (rowt_hi, rowt_lo))
                        src = bank[4 + (1 + p0 + i) % 2][:, :].rearrange("p (k b c) -> p k b c", k=4, c=C)
                        dve.tensor_copy(hi, src).then_inc(t2_hi, 1)
                        dve.wait_ge(t2_hi, a * T2J + i + 1)
                        dve.tensor_tensor(lo, src, hi, ALU.subtract).then_inc(t2_out, 1)

                    if head:
                        dve.wait_ge(y_done, a * YJ + 1)
                    if tail_:
                        dve.wait_ge(x_done, (a - 1) * XJ + 1)
                    for i in range(YJ):
                        if head:
                            for j in (2 * i, 2 * i + 1):
                                dve.wait_ge(t_hi, (a + 1) * TJ + j + 1)
                                rows_lo(par, j)
                        if tail_ and i < T2J:
                            t2(i)
                    if tail_:
                        for i in range(XJ):
                            dve.wait_ge(x_done, a * XJ + i + 2)
                            dve.tensor_copy(spec_flat[:, bass.ds((g - 1) * (GI * SPEC) + i * 288, 288)], bank[6 + i][:, 0:288])\
                               .then_inc(x_out, 1)
                pipelined(dve, step)

            def mix_weights(l):
                dve.wait_ge(bd_zero, l + 1)
                alone(dve)

                def step(c, h, par):
                    m = l * NCH + c
                    dve.wait_ge(wd_in[par], (l * (NCH // 2) + h + 1) * 16)
                    reuse(dve, mix_done, MJ, m)
                    for j in range(KY4):
                        r = slice(j * C, (j + 1) * C)
                        dve.tensor_copy(bd[par][r, :, 0:2, j * C:(j + 1) * C], wds[par][r, :, :, :])
                        ins = dve.tensor_scalar(bd[par][r, :, 2, j * C:(j + 1) * C], wds[par][r, :, 1, :], -1.0, None, ALU.mult)
                    ins.then_inc(bd_ready, 1)
                by_pairs(dve, l, NCH, step)

            def inverse(l):
                def step(g, h, par, head, tail_):
                    n = l * NG + g
                    p0 = 1 - par

                    def count(i):
                        dve.wait_ge(fin_out, (n - 1) * FJ + i + 1)
                        dve.bn_stats(stats[:, bass.ds((g - 1) * (FJ * 6) + i * 6, 6)], pix[p0][:, i * 512:(i + 1) * 512])\
                           .then_inc(stats_done, 1)

                    def t3(i):
                        dve.wait_ge(t3_done, n * T3J + i + 1)
                        dst = kxt[par][:, i * 512:(i + 1) * 512].rearrange("p (k b o) -> p b k o", k=4, o=C)
                        src = bank[(par + i) % 2][0:96, 0:256].bitcast(F16).rearrange("p (b k o) -> p b k o", k=4, o=C)
                        dve.tensor_copy(dst, src).then_inc(t3_out, 1)

                    def xi(i):
                        dve.wait_ge(xi_hi, n * XIJ + i + 1)
                        src = bank[2 + (par + i) % 2][:, :].rearrange("p (k x r) -> p k x r", k=4, r=2)
                        k = slice(4 * i, 4 * i + 4)
                        dve.tensor_tensor(xrows[par][:, 1, k], src, xrows[par][:, 0, k], ALU.subtract).then_inc(xi_out, 1)

                    def t4(i):
                        dve.wait_ge(t4_done, n * T4J + i + 1)
                        dve.tensor_copy(ht[par][:, 8 * i:8 * i + 8, :].rearrange("p q n -> p (q n)"), bank[4 + i % 2][0:96, :].bitcast(F16))\
                           .then_inc(t4_out, 1)

                    if head:
                        reuse(dve, xi_done, XIJ, n)
                        reuse(dve, fin_done, FJ, n)
                    inverse_order(head, tail_, t3=t3, xi=xi, t4=t4, final=count)
                pipelined(dve, step, isinstance(l, int))

            def normalise(l):
                base = l * BN_STEPS
                done = [0]

                def step(ins):
                    done[0] += 1
                    ins.then_inc(bn_step, 1)
                    dve.wait_ge(bn_step, base + done[0])

                dve.wait_ge(stats_done, (l + 1) * (NG * FJ))
                alone(dve)
                step(dve.bn_aggr(bn[:, 0:2], stats[:, :]))
                step(dve.tensor_copy(bn[:, 2:3], bn[:, 0:1]))
                step(dve.scalar_tensor_tensor(bn[:, 3:4], bn[:, 0:1], bn[:, 0:1], bn[:, 1:2], ALU.mult, ALU.add))
                dve.wait_ge(bn_avg, l + 1)
                step(dve.tensor_copy(bn[:, 4:6], bank[0][:, 0:2]))
                step(dve.scalar_tensor_tensor(bn[:, 7:8], bn[:, 4:5], bn[:, 4:5], bn[:, 5:6], ALU.mult, ALU.subtract))
                step(dve.tensor_scalar(bn[:, 8:9], bn[:, 7:8], -1.0, EPS, ALU.mult, ALU.add))
                dve.wait_ge(bn_sqrt, l + 1)
                step(dve.reciprocal(bn[:, 10:11], bn[:, 9:10]))
                step(dve.scalar_tensor_tensor(bn[:, 11:12], bn[:, 10:11], bn[:, 10:11], bn[:, 8:9], ALU.mult, ALU.mult))
                step(dve.tensor_scalar(bn[:, 12:13], bn[:, 11:12], -0.5, 1.5, ALU.mult, ALU.add))
                step(dve.tensor_tensor(bn[:, 13:14], bn[:, 10:11], bn[:, 12:13], ALU.mult))
                step(dve.tensor_tensor(scale_l, bn[:, 13:14], gamma, ALU.mult))
                step(dve.scalar_tensor_tensor(bn[:, 14:15], bn[:, 4:5], scale_l, beta, ALU.mult, ALU.subtract))
                step(dve.tensor_scalar(bias_l, bn[:, 14:15], -1.0, None, ALU.mult))
                assert done[0] == BN_STEPS

            def layer_constants(l):
                dve.tensor_copy(wcur[:, :], wm[:, l, :])
                dve.tensor_copy(bn[:, 18:20], chan_sb[:, l, 1:3])
                dve.tensor_copy(wb, chan_sb[:, l, 0:1]).then_inc(w_ready, 1)

            first_forward()
            dve.tensor_copy(bn[:, 18:20], chan_sb[:, 0, 1:3])
            dve.tensor_copy(wb, chan_sb[:, 0, 0:1])
            mix_weights(0)
            dve.wait_ge(w7_done, 1)
            dve.tensor_copy(wx7[:, :], bank[2][0:96, 0:P]).then_inc(w7_hi, 1)
            dve.wait_ge(w7_hi, 1)
            dve.tensor_tensor(wx7[64:96, :], bank[2][64:96, 0:P], wx7[64:96, :], ALU.subtract).then_inc(w7_ready, 1)
            inverse(0)
            normalise(0)
            with dve.Fori(1, L) as l:
                forward(l)
                layer_constants(l)
                mix_weights(l)
                inverse(l)
                normalise(l)

            dve.tensor_scalar(bn[:, 22:23], qbd_sb[:, GI:GI + 1], bias_l, None, ALU.mult).then_inc(q_step, 1)
            dve.wait_ge(q_sum, 1)
            dve.tensor_scalar(hconst, bank[4][:, 0:1], qb_sb[:, 0:1], None, ALU.add)
            dve.tensor_scalar(qcol[:, :], qbd_sb[:, 0:GI], scale_l, None, ALU.mult).then_inc(q_ready, 1)

            for q in range(2):
                dve.wait_ge(u_stored[q], L * HG * 16)

            def step(g, h, par, head, tail_):
                if head:
                    if not isinstance(g, int) or g >= 2:
                        dve.wait_ge(h_stored[par], h * 16)
                    for i in range(1, FJ, 2):
                        dve.wait_ge(head_done, g * FJ + i + 1)
                        dve.tensor_scalar(pix[par][0:GI, i * 512:(i + 1) * 512], bank[i][0:GI, :], hconst[0:GI, :],
                                          None, ALU.add).then_inc(head_out[1], 1)
            pipelined(dve, step, True)
            tok_vector(dve)

NTOK = B * S
NT = NTOK // P
D = S
H, HD = 8, 8
WS2 = 49
PAD = S - WS2
TAB = 13 * 13
NIDX = WS2 * WS2
NE, FF = 16, 128
NI = NT // 2
EH = NE // 2
LN_STEPS = 10


def four_stages(eng, step):
    step(0, 0, (True, False, False, False))
    step(1, 1, (True, True, False, False))
    step(2, 0, (True, True, True, False))
    step(3, 1, (True, True, True, True))
    with eng.Fori(2, NT // 2) as i:
        step(i * 2, 0, (True, True, True, True))
        step(i * 2 + 1, 1, (True, True, True, True))
    step(NT, 0, (False, True, True, True))
    step(NT + 1, 1, (False, False, True, True))
    step(NT + 2, 0, (False, False, False, True))


def token_programs(nc, ctx, bank, sem, h_dram, h_stored, att, moe, out):
    bias_dram = nc.dram_tensor("rel_bias", [H, WS2, WS2], F32, kind="Internal").ap()

    def pair(name):
        return [sem(f"{name}{s}") for s in range(2)]

    def sb(name, shape, dt=F32):
        return ctx.enter_context(nc.sbuf_tensor(name, shape, dt))

    consts = []

    def const(name, src):
        t = sb(name, list(src.shape), src.dtype)
        consts.append((t, src))
        return t

    h = sb("h", [P, NT, D])
    xn = sb("xn", [P, NT, D])
    sq = sb("sq", [P, NT, D])
    ln = sb("ln", [P, 8, NT])
    idn = const("t_ident", att["ident"])
    wqk = const("wqk", att["wqk"])
    wv = const("wv", att["wv"])
    wp = const("wp", att["wp"])
    head_mask = const("head_mask", att["head_mask"])
    v_mask = const("v_mask", att["v_mask"])
    iota = const("iota", att["iota"])
    tab = [const("tab0", att["table"][0:P, :]), const("tab1", att["table"][P:TAB, :])]
    gw = const("gw", moe["gw"])
    gb = const("gb", moe["gb"])
    w1 = const("w1", moe["w1"])
    b1 = const("b1", moe["b1"])
    w2 = const("w2", moe["w2"])
    gw_hi, gw_lo = sb("gw_hi", [P, NE], F16), sb("gw_lo", [P, NE], F16)
    w1_hi, w1_lo = sb("w1_hi", [P, NE * FF], F16), sb("w1_lo", [P, NE * FF], F16)
    w2_hi, w2_lo = sb("w2_hi", [P, NE * D], F16), sb("w2_lo", [P, NE * D], F16)
    b1_16 = sb("b1_16", [33, NE * FF], F16)
    ones = sb("ones", [33, 2 * P], F16)
    b2 = const("b2", moe["b2"])
    gamma = const("gamma", moe["gamma"])
    beta = const("beta", moe["beta"])
    erow = const("erow", moe["erow"])
    idx = sb("idx", [P, NIDX], I32)
    idxf = sb("idxf", [P, NIDX])
    hot = [sb(f"hot{s}", [P, NIDX]) for s in range(2)]
    bias_rows = sb("bias_rows", [H, NIDX])
    bias = sb("bias", [P, H, S])
    xc = [sb(f"xc{s}", [P, D]) for s in range(2)]
    xT = [sb(f"xT{s}", [D, 2, 2, S]) for s in range(2)]
    qd = [sb(f"qd{s}", [P, P]) for s in range(2)]
    ks = [sb(f"ks{s}", [P, S]) for s in range(2)]
    kd = [sb(f"kd{s}", [P, H, S]) for s in range(2)]
    vd = [sb(f"vd{s}", [P, 2, D]) for s in range(2)]
    sc = [sb(f"sc{s}", [P, H, S]) for s in range(2)]
    mx = [sb(f"mx{s}", [P, H]) for s in range(2)]
    sm = [sb(f"sm{s}", [P, H]) for s in range(2)]
    rs = [sb(f"rs{s}", [P, H]) for s in range(2)]
    pT = [sb(f"pT{s}", [P, 4, P]) for s in range(2)]
    o = [sb(f"o{s}", [P, D]) for s in range(2)]
    oT = [sb(f"oT{s}", [D + 1, P]) for s in range(2)]
    x16 = sq[:, :, :].rearrange("p t y -> p (t y)").bitcast(F16).rearrange("p (t i y) -> p t i y", i=2, y=D)
    xTs = sb("xTs", [P, NTOK], F16)
    lg = sb("lg", [P, NT, NE])
    top = sb("top", [P, NT, 8])
    topi = sb("topi", [P, NT, 8], U32)
    gv = sb("gv", [P, 6, NT])
    gate = sb("gate", [P, NT, NE])
    gate2 = sb("gate2", [P, NT, NE])
    gT = sb("gT", [P, NT // 8, P])
    hid_hi = [sb(f"hid_hi{s}", [P, 2, 2 * P], F16) for s in range(4)]
    hid_lo = [sb(f"hid_lo{s}", [P, 2, 2 * P], F16) for s in range(4)]
    idn16 = const("t_ident16", att["ident16"])
    wo = [t[:, 0:NE * D].rearrange("p (a n) -> p a n", a=2) for t in hot]

    c_in, idx_in, h_in, out_st = sem("c_in"), sem("idx_in"), sem("h_in"), sem("out_st")
    cleared, t_waited = sem("cleared"), sem("t_waited")
    ln_step, ln_sq, ln_sqrt = sem("ln_step"), sem("ln_sq"), sem("ln_sqrt")
    hot_ready, rb_done, rb_out, rb_stored, bias_in = (sem("hot_ready"), sem("rb_done"), sem("rb_out"),
                                                      sem("rb_stored"), sem("bias_in"))
    xc_ready, xt_done, xt_out = sem("xc_ready"), sem("xt_done"), sem("xt_out")
    qk_done, qk_out, kd_ready = sem("qk_done"), sem("qk_out"), sem("kd_ready")
    v_done, v_out = sem("v_done"), sem("v_out")
    s_done, s_out, mx_done, sub_done, exp_done, sum_done, rs_done = (
        sem("s_done"), sem("s_out"), sem("mx_done"), sem("sub_done"), sem("exp_done"), sem("sum_done"), sem("rs_done"))
    pt_done, pt_out, av_done, o_out = sem("pt_done"), sem("pt_out"), sem("av_done"), sem("o_out")
    ot_done, ot_out, pr_done, pr_out = sem("ot_done"), sem("ot_out"), sem("pr_done"), sem("pr_out")
    x_ready, mt_done, mt_out, lg_done, lg_out = (sem("x_ready"), sem("mt_done"), sem("mt_out"), sem("lg_done"),
                                                 sem("lg_out"))
    top_done, gap_ready, gap_exp, gate_step = sem("top_done"), sem("gap_ready"), sem("gap_exp"), sem("gate_step")
    gt_done, gt_out, b2_done, b2_out = sem("gt_done"), sem("gt_out"), sem("b2_done"), sem("b2_out")
    hid_done, hid_top, hid_out, hid_used = sem("hid_done"), sem("hid_top"), sem("hid_out"), sem("hid_used")
    w_hi, w_split, x_hi, x_split = sem("w_hi"), sem("w_split"), sem("x_hi"), sem("x_split")
    eo_done, eo_out, sum_step, moe_sum = sem("eo_done"), sem("eo_out"), sem("sum_step"), sem("moe_sum")
    fin_step = sem("fin_step")
    C_IN = 16 * len(consts)
    GATE_STEPS, FIN_STEPS = 8, 4
    NCLEAR = 6
    NSPLIT = 4
    HJ = 8
    RB = [(i * 512, min(512, NIDX - i * 512)) for i in range(-(-NIDX // 512))]

    def apart(eng):
        eng.sem_inc(t_waited, 1)

    def tile(t3, t):
        return t3[:, bass.ds(t, 1), :].rearrange("p t y -> p (t y)")

    def sync(sp):
        for s in range(2):
            sp.wait_ge(h_stored[s], 16 * HG)
        for t, src in consts:
            sp.dma_start(t[:], src).then_inc(c_in, 16)
        sp.dma_start(idx[:, :], att["index"].broadcast_to([P, NIDX])).then_inc(idx_in, 16)
        sp.dma_start(h[:, :, :], h_dram.rearrange("g i (n y) -> (g i n) y", y=D).rearrange("(t p) y -> p t y", p=P))\
          .then_inc(h_in, 16)
        sp.wait_ge(rb_out, len(RB))
        sp.dma_start(bias_dram.rearrange("h n m -> h (n m)"), bias_rows[:, :]).then_inc(rb_stored, 16)
        sp.wait_ge(rb_stored, 16)
        sp.wait_ge(cleared, NCLEAR)
        for i in range(2):
            sp.dma_start(bias[i * S + PAD:(i + 1) * S, :, PAD:S], bias_dram.rearrange("h n m -> n h m")).then_inc(bias_in, 16)
        sp.wait_ge(fin_step, FIN_STEPS + 1)
        sp.dma_start(out.rearrange("b n y -> (b n) y").rearrange("(t p) y -> p t y", p=P), h[:, :, :]).then_inc(out_st, 16)
        sp.wait_ge(out_st, 16)

    def gpsimd(gp):
        for s in range(2):
            gp.wait_ge(h_stored[s], 16 * HG)
        gp.memset(bias[:, :, :], 0.0).then_inc(cleared, 1)
        for s in range(2):
            gp.memset(qd[s][:, :], 0.0).then_inc(cleared, 1)
            gp.memset(oT[s][:, :], 1.0).then_inc(cleared, 1)
        gp.memset(ones[:, :], 1.0).then_inc(cleared, 1)
        gp.wait_ge(c_in, C_IN)

        def step(t, par, on):
            if on[1]:
                p1 = 1 - par
                gp.wait_ge(mx_done, t)
                gp.tensor_tensor(sc[p1][:, :, :], sc[p1][:, :, :], mx[p1][:, :].unsqueeze(2).to_broadcast([P, H, S]),
                                 ALU.subtract).then_inc(sub_done, 1)
            if on[0]:
                gp.wait_ge(qk_out, (t + 1) * 2)
                reuse(gp, s_done, 1, t)
                gp.tensor_tensor(kd[par][:, :, :], ks[par][:, :].unsqueeze(1).to_broadcast([P, H, S]),
                                 head_mask[:, :].unsqueeze(2).to_broadcast([P, H, S]), ALU.mult).then_inc(kd_ready, 1)
        four_stages(gp, step)

        gp.tensor_copy(gw_hi[:, :], gw[:, :]).then_inc(w_hi, 1)
        gp.tensor_copy(w1_hi[:, :], w1[:, :]).then_inc(w_hi, 1)
        gp.tensor_copy(w2_hi[:, :], w2[:, :]).then_inc(w_hi, 1)
        gp.tensor_copy(b1_16[:, :], b1[:, :]).then_inc(w_hi, 1)
        gp.wait_ge(w_hi, NSPLIT)
        gp.tensor_tensor(gw_lo[:, :], gw[:, :], gw_hi[:, :], ALU.subtract).then_inc(w_split, 1)
        gp.tensor_tensor(w1_lo[:, :], w1[:, :], w1_hi[:, :], ALU.subtract).then_inc(w_split, 1)
        gp.tensor_tensor(w2_lo[:, :], w2[:, :], w2_hi[:, :], ALU.subtract).then_inc(w_split, 1)
        gp.wait_ge(w_split, NSPLIT - 1)
        gp.tensor_tensor(b1_16[32:33, :], b1[32:33, :], b1_16[32:33, :], ALU.subtract).then_inc(w_split, 1)

        def turn(it):
            for q in range(2):
                n = it * 2 + q
                w = wo[q][:, :, :].rearrange("p a n -> p (a n)")
                gp.wait_ge(eo_out, it * 4 + 3 + q)
                width = NE * D // 2
                done = 0
                while width > D:
                    gp.tensor_tensor(w[:, 0:width], w[:, 0:width], w[:, width:2 * width], ALU.add).then_inc(sum_step, 1)
                    done += 1
                    gp.wait_ge(sum_step, n * 3 + done)
                    width //= 2
                gp.tensor_tensor(tile(sq, n), w[:, 0:D], w[:, D:2 * D], ALU.add).then_inc(moe_sum, 1)
        with gp.Fori(0, NI) as it:
            turn(it)

    def tensor(pe):
        pe.wait_ge(c_in, C_IN)
        pe.wait_ge(hot_ready, 2)
        for i, (at, n) in enumerate(RB):
            bank_free(pe, rb_out, i)
            pe.matmul(bank[i % 2][0:H, 0:n], tab[0][:, :], hot[0][:, at:at + n], start=True, stop=False)
            pe.matmul(bank[i % 2][0:H, 0:n], tab[1][:, :], hot[1][0:TAB - P, at:at + n], start=False, stop=True)\
              .then_inc(rb_done, 1)
        pe.wait_ge(rb_out, len(RB))
        pe.wait_ge(cleared, NCLEAR)

        def step(t, par, on):
            a, b, c, d = on
            p1 = 1 - par

            def features():
                pe.wait_ge(xc_ready, t + 1)
                bank_free(pe, xt_out, t, 1)
                apart(pe)
                pe.transpose(bank[0][0:D, 0:P], xc[par][:, :], idn[:, :]).then_inc(xt_done, 1)

            def projections():
                pe.wait_ge(xt_out, t + 1)
                bank_free(pe, qk_out, t * 2, 1)
                rhs = xT[par][:, :, 0, :]
                pe.matmul(bank[1][:, 0:P], wqk[:, 0:P], rhs, start=True, stop=True)
                pe.matmul(bank[1][:, P:2 * P], wqk[:, P:2 * P], rhs, start=True, stop=True).then_inc(qk_done, 1)
                bank_free(pe, v_out, t, 1)
                for i in range(2):
                    mm = pe.matmul(bank[2][:, i * D:(i + 1) * D], xT[par][:, i, :, :].rearrange("p c n -> p (c n)"),
                                   wv[:, :], start=True, stop=True)
                mm.then_inc(v_done, 1)

            def scores():
                pe.wait_ge(kd_ready, t)
                bank_free(pe, s_out, t - 1, 1)
                pe.matmul(bank[3][:, :], qd[p1][:, :], kd[p1][:, :, :].rearrange("p h m -> p (h m)"),
                          start=True, stop=True).then_inc(s_done, 1)

            def turned():
                pe.wait_ge(exp_done, t - 1)
                bank_free(pe, pt_out, t - 2, 1)
                for i in range(4):
                    mm = pe.transpose(bank[4][:, i * P:(i + 1) * P], sc[par][:, 2 * i:2 * i + 2, :].rearrange("p h m -> p (h m)"),
                                      idn[:, :])
                mm.then_inc(pt_done, 1)

            def values():
                pe.wait_ge(pt_out, t - 1)
                pe.wait_ge(v_out, t - 1)
                bank_free(pe, o_out, t - 2, 1)
                for i in range(2):
                    for j in range(4):
                        mm = pe.matmul(bank[5][i * S:(i + 1) * S, j * 16:(j + 1) * 16], pT[par][:, j, i * S:(i + 1) * S],
                                       vd[par][:, i, j * 16:(j + 1) * 16], start=True, stop=True)
                mm.then_inc(av_done, 1)

            def joined():
                pe.wait_ge(o_out, t - 1)
                bank_free(pe, ot_out, t - 2, 1)
                apart(pe)
                pe.transpose(bank[6][0:D, 0:P], o[par][:, :], idn[:, :]).then_inc(ot_done, 1)

            def projected():
                pe.wait_ge(ot_out, t - 2)
                bank_free(pe, pr_out, t - 3, 1)
                pe.matmul(bank[7][:, 0:D], oT[p1][:, :], wp[:, :], start=True, stop=True).then_inc(pr_done, 1)

            if a:
                features()
            if c:
                turned()
            if b:
                scores()
            if d:
                projected()
            if c:
                values()
            if a:
                projections()
            if c:
                joined()
        four_stages(pe, step)

        pe.wait_ge(w_split, NSPLIT)
        pe.wait_ge(x_split, 1)
        for t in range(NT):
            n, q = divmod(t, 4)
            if q == 0:
                bank_free(pe, mt_out, n)
            mm = pe.transpose(bank[n % 2][:, 0:256].bitcast(F16)[:, q * P:(q + 1) * P],
                              x16[:, t, :, :].rearrange("p i y -> p (i y)"), idn16[:, :])
            if q == 3:
                mm.then_inc(mt_done, 1)
                if n % 2:
                    pe.wait_ge(mt_out, n + 1)
                    bank_free(pe, lg_out, n // 2)
                    for r in range(8):
                        tt = t - 7 + r
                        logits = bank[2 + n // 2 % 2][:, r * NE:(r + 1) * NE]
                        pe.matmul(logits, xTs[:, tt * P:(tt + 1) * P], gw_hi[:, :], start=True, stop=False)
                        mm = pe.matmul(logits, xTs[:, tt * P:(tt + 1) * P], gw_lo[:, :], start=False, stop=True)
                    mm.then_inc(lg_done, 1)
        pe.wait_ge(gate_step, GATE_STEPS)
        for n in range(NT // 8):
            bank_free(pe, gt_out, n)
            pe.transpose(bank[4 + n % 2][:, 0:P], gate[:, 8 * n:8 * n + 8, :].rearrange("p t e -> p (t e)"), idn[:, :])\
              .then_inc(gt_done, 1)
            pe.wait_ge(gt_out, n + 1)
            bank_free(pe, b2_out, n)
            pe.matmul(bank[6 + n % 2][:, :], gT[:, n, :], b2[:, :], start=True, stop=True).then_inc(b2_done, 1)
        pe.wait_ge(b2_out, NT // 8)

        def hidden(it, j):
            if not isinstance(it, int) or it * HJ + j >= 4:
                pe.wait_ge(hid_out, it * HJ + j - 3)
            for i in range(2):
                e = 2 * j + i
                f = slice(e * FF, (e + 1) * FF)
                acc = bank[j % 4][:, i * 2 * P:(i + 1) * 2 * P]
                x = xTs[:, bass.ds(it * (2 * P), 2 * P)]
                pe.matmul(acc, w1_hi[:, f], x, start=True, stop=False)
                pe.matmul(acc, w1_lo[:, f], x, start=False, stop=False)
                mm = pe.matmul(acc, b1_16[:, f], ones[:, :], start=False, stop=True)
            mm.then_inc(hid_done, 1)

        def turn(it, ahead=True):
            now = not isinstance(it, int)

            def output(j):
                half = j // 4
                if j % 4 == 0 and (now or it):
                    pe.wait_ge(eo_out, it * 4 - 2 + 2 * half)
                pe.wait_ge(hid_out, it * HJ + j + 1)
                for i in range(2):
                    e = 2 * j + i
                    for q in range(2):
                        acc = bank[4 + 2 * half + q][:, (e % EH) * D:(e % EH + 1) * D]
                        hi, lo = (t[j % 4][:, i, q * P:(q + 1) * P] for t in (hid_hi, hid_lo))
                        y = slice(e * D, (e + 1) * D)
                        pe.matmul(acc, hi, w2_hi[:, y], start=True, stop=False)
                        pe.matmul(acc, hi, w2_lo[:, y], start=False, stop=False)
                        mm = pe.matmul(acc, lo, w2_hi[:, y], start=False, stop=True)
                mm.then_inc(hid_used, 1)

            for j in range(HJ):
                output(j)
                if j + 3 < HJ:
                    hidden(it, j + 3)
                elif ahead:
                    hidden(it + 1, j + 3 - HJ)

        for j in range(3):
            hidden(0, j)
        turn(0)
        with pe.Fori(1, NI - 1) as it:
            turn(it)
        turn(NI - 1, ahead=False)

    def layer_norm_act(act, use):
        act.wait_ge(ln_step, use * LN_STEPS + 3)
        act.activation(sq[:, :, :], xn[:, :, :], ACT.Square).then_inc(ln_sq, 1)
        act.wait_ge(ln_step, use * LN_STEPS + 5)
        act.activation(ln[:, 3, :], ln[:, 2, :], ACT.Sqrt).then_inc(ln_sqrt, 1)

    def scalar(act):
        act.wait_ge(c_in, C_IN)
        for i, (at, n) in enumerate(RB):
            act.wait_ge(rb_done, i + 1)
            act.copy(bias_rows[:, at:at + n], bank[i % 2][0:H, 0:n]).then_inc(rb_out, 1)
        layer_norm_act(act, 0)
        act.wait_ge(ln_step, LN_STEPS)
        act.wait_ge(cleared, NCLEAR)

        def step(t, par, on):
            a, b, c, d = on
            p1 = 1 - par
            if a:
                reuse(act, xt_done, 1, t)
                act.activation(xc[par][:, :], tile(xn, t), ACT.Copy, scale=ln[:, 7, bass.ds(t, 1)]).then_inc(xc_ready, 1)
            if d:
                act.wait_ge(ot_done, t - 2)
                reuse(act, pr_done, 1, t - 3)
                act.copy(oT[p1][0:D, :], bank[6][0:D, 0:P]).then_inc(ot_out, 1)
            if c:
                act.wait_ge(pt_done, t - 1)
                reuse(act, av_done, 1, t - 2)
                act.copy(pT[par][:, :, :].rearrange("p i n -> p (i n)"), bank[4][:, :]).then_inc(pt_out, 1)
            if a:
                act.wait_ge(xt_done, t + 1)
                reuse(act, v_done, 1, t)
                act.copy(xT[par][:, :, :, :],
                         bank[0][0:D, 0:P].rearrange("p (i n) -> p i n", i=2).unsqueeze(2).to_broadcast([D, 2, 2, S]))\
                   .then_inc(xt_out, 1)
                act.wait_ge(qk_done, t + 1)
                reuse(act, s_done, 1, t)
                for i in range(2):
                    r = slice(i * D, (i + 1) * D)
                    act.copy(qd[par][r, i * S:(i + 1) * S], bank[1][r, i * S:(i + 1) * S])
                    ins = act.copy(ks[par][r, :], bank[1][r, P + i * S:P + (i + 1) * S])
                    ins.then_inc(qk_out, 1)
            if b:
                act.wait_ge(sub_done, t)
                px = sc[p1][:, :, :]
                act.activation(px, px, ACT.Exp).then_inc(exp_done, 1)
        four_stages(act, step)

        layer_norm_act(act, 1)
        act.wait_ge(x_ready, 1)
        act.copy(x16[:, :, 0, :], xn[:, :, :]).then_inc(x_hi, 1)
        for n in range(NT // 4):
            act.wait_ge(mt_done, n + 1)
            act.copy(xTs[:, n * 512:(n + 1) * 512], bank[n % 2][:, 0:256].bitcast(F16)).then_inc(mt_out, 1)
        act.wait_ge(gap_ready, 1)
        act.activation(gv[:, 1, :], gv[:, 0, :], ACT.Exp).then_inc(gap_exp, 1)

        def turn(it):
            for j in range(HJ):
                act.wait_ge(hid_done, it * HJ + j + 1)
                if not isinstance(it, int) or j >= 4:
                    act.wait_ge(hid_used, it * HJ + j - 3)
                act.activation(hid_hi[j % 4][:, :, :].rearrange("p i n -> p (i n)"), bank[j % 4][:, :], ACT.Relu)\
                   .then_inc(hid_top, 1)
        turn(0)
        with act.Fori(1, NI) as it:
            turn(it)
        layer_norm_act(act, 2)

    def layer_norm(dve, use, src):
        done = [use * LN_STEPS]

        def step(ins):
            done[0] += 1
            ins.then_inc(ln_step, 1)
            dve.wait_ge(ln_step, done[0])

        step(dve.reduce_sum(ln[:, 0, :], src[:, :, :], AX.X))
        step(dve.tensor_scalar(ln[:, 1, :], ln[:, 0, :], 1.0 / D, None, ALU.mult))
        step(dve.tensor_tensor(xn[:, :, :], src[:, :, :], ln[:, 1, :].unsqueeze(2).to_broadcast([P, NT, D]), ALU.subtract))
        dve.wait_ge(ln_sq, use + 1)
        step(dve.reduce_sum(ln[:, 0, :], sq[:, :, :], AX.X))
        step(dve.tensor_scalar(ln[:, 2, :], ln[:, 0, :], 1.0 / D, EPS, ALU.mult, ALU.add))
        dve.wait_ge(ln_sqrt, use + 1)
        step(dve.reciprocal(ln[:, 4, :], ln[:, 3, :]))
        step(dve.tensor_tensor(ln[:, 5, :], ln[:, 4, :], ln[:, 4, :], ALU.mult))
        step(dve.tensor_tensor(ln[:, 5, :], ln[:, 5, :], ln[:, 2, :], ALU.mult))
        step(dve.tensor_scalar(ln[:, 6, :], ln[:, 5, :], -0.5, 1.5, ALU.mult, ALU.add))
        step(dve.tensor_tensor(ln[:, 7, :], ln[:, 4, :], ln[:, 6, :], ALU.mult))

    def vector(dve):
        dve.wait_ge(c_in, C_IN)
        dve.wait_ge(idx_in, 16)
        dve.tensor_copy(idxf[:, :], idx[:, :]).then_inc(top_done, 1)
        dve.wait_ge(top_done, 1)
        for i in range(2):
            dve.tensor_scalar(hot[i][:, :], idxf[:, :], iota[:, i:i + 1], None, ALU.is_equal).then_inc(hot_ready, 1)
        dve.wait_ge(h_in, 16)
        layer_norm(dve, 0, h)
        dve.wait_ge(bias_in, 32)

        def step(t, par, on):
            a, b, c, d = on
            p1 = 1 - par
            if b:
                dve.wait_ge(s_done, t)
                if not isinstance(t, int) or t >= 3:
                    dve.wait_ge(pt_done, t - 2)
                dve.scalar_tensor_tensor(sc[p1][:, :, :].rearrange("p h m -> p (h m)"), bank[3][:, :], HD ** -0.5,
                                         bias[:, :, :].rearrange("p h m -> p (h m)"), ALU.mult, ALU.add).then_inc(s_out, 1)
                dve.wait_ge(s_out, t)
                dve.reduce_max(mx[p1][:, :], sc[p1][:, :, :], AX.X).then_inc(mx_done, 1)
            if c:
                dve.wait_ge(exp_done, t - 1)
                dve.reduce_sum(sm[par][:, :], sc[par][:, :, :], AX.X).then_inc(sum_done, 1)
                dve.wait_ge(sum_done, t - 1)
                dve.reciprocal(rs[par][:, :], sm[par][:, :]).then_inc(rs_done, 1)
            if d:
                dve.wait_ge(pr_done, t - 2)
                ht_ = tile(h, t - 3)
                dve.tensor_tensor(ht_, bank[7][:, 0:D], ht_, ALU.add).then_inc(pr_out, 1)
            if c:
                dve.wait_ge(av_done, t - 1)
                dve.wait_ge(rs_done, t - 1)
                reuse(dve, ot_done, 1, t - 2)
                dve.tensor_tensor(o[par][:, :].rearrange("p (h d) -> p h d", h=H), bank[5][:, 0:D].rearrange("p (h d) -> p h d", h=H),
                                  rs[par][:, :].unsqueeze(2).to_broadcast([P, H, HD]), ALU.mult).then_inc(o_out, 1)
            if a:
                dve.wait_ge(v_done, t + 1)
                reuse(dve, av_done, 1, t)
                dve.tensor_tensor(vd[par][:, :, :].rearrange("p i n -> p (i n)"), bank[2][:, 0:P], v_mask[:, :], ALU.mult)\
                   .then_inc(v_out, 1)
        four_stages(dve, step)

        dve.wait_ge(pr_out, NT)
        layer_norm(dve, 1, h)
        dve.tensor_tensor(xn[:, :, :], xn[:, :, :], ln[:, 7, :].unsqueeze(2).to_broadcast([P, NT, D]), ALU.mult).then_inc(x_ready, 1)
        dve.wait_ge(x_hi, 1)
        dve.tensor_tensor(x16[:, :, 1, :], xn[:, :, :], x16[:, :, 0, :], ALU.subtract).then_inc(x_split, 1)
        for n in range(NT // 8):
            dve.wait_ge(lg_done, n + 1)
            dve.tensor_tensor(lg[:, 8 * n:8 * n + 8, :], bank[2 + n % 2][:, 0:8 * NE].rearrange("p (t e) -> p t e", e=NE),
                              gb[:, :].unsqueeze(1).to_broadcast([P, 8, NE]), ALU.add).then_inc(lg_out, 1)
        dve.wait_ge(lg_out, NT // 8)
        for t in range(NT):
            dve.max(top[:, t, :], lg[:, t, :]).then_inc(top_done, 1)
        dve.wait_ge(top_done, NT + 1)
        for t in range(NT):
            dve.max_index(topi[:, t, :], top[:, t, :], lg[:, t, :]).then_inc(top_done, 1)

        dve.tensor_tensor(gv[:, 0, :], top[:, :, 1], top[:, :, 0], ALU.subtract).then_inc(gap_ready, 1)
        dve.wait_ge(top_done, 2 * NT + 1)
        done = [0]

        def gstep(ins):
            done[0] += 1
            ins.then_inc(gate_step, 1)
            dve.wait_ge(gate_step, done[0])

        full = [P, NT, NE]
        gstep(dve.tensor_copy(gv[:, 4:6, :].rearrange("p i t -> p t i"), topi[:, :, 0:2]))
        dve.wait_ge(gap_exp, 1)
        gstep(dve.tensor_scalar(gv[:, 2, :], gv[:, 1, :], 1.0, None, ALU.add))
        gstep(dve.reciprocal(gv[:, 2, :], gv[:, 2, :]))
        gstep(dve.tensor_tensor(gv[:, 3, :], gv[:, 2, :], gv[:, 1, :], ALU.mult))
        er = erow[:, :].unsqueeze(1).to_broadcast(full)
        dve.tensor_tensor(gate[:, :, :], er, gv[:, 4, :].unsqueeze(2).to_broadcast(full), ALU.is_equal)
        gstep(dve.tensor_tensor(gate2[:, :, :], er, gv[:, 5, :].unsqueeze(2).to_broadcast(full), ALU.is_equal))
        gstep(dve.tensor_tensor(gate[:, :, :], gate[:, :, :], gv[:, 2, :].unsqueeze(2).to_broadcast(full), ALU.mult))
        gstep(dve.tensor_tensor(gate2[:, :, :], gate2[:, :, :], gv[:, 3, :].unsqueeze(2).to_broadcast(full), ALU.mult))
        gstep(dve.tensor_tensor(gate[:, :, :], gate[:, :, :], gate2[:, :, :], ALU.add))
        assert done[0] == GATE_STEPS
        for n in range(NT // 8):
            dve.wait_ge(gt_done, n + 1)
            dve.tensor_copy(gT[:, n, :], bank[4 + n % 2][:, 0:P]).then_inc(gt_out, 1)
            dve.wait_ge(b2_done, n + 1)
            part = xn[:, 8 * n:8 * n + 8, :].rearrange("p t y -> p (t y)")
            dve.tensor_tensor(part, bank[6 + n % 2][:, :], part, ALU.add).then_inc(b2_out, 1)

        def turn(it):
            now = not isinstance(it, int)

            def gated(half):
                for q in range(2):
                    if now and half == 0:
                        dve.wait_ge(moe_sum, it * 2 - 1 + q)
                    dve.wait_ge(hid_used, it * HJ + 4 * half + 4)
                    dve.tensor_tensor(wo[q][:, half, :].rearrange("p (e y) -> p e y", y=D),
                                      bank[4 + 2 * half + q][:, :].rearrange("p (e y) -> p e y", y=D),
                                      gate[:, bass.ds(it * 2 + q, 1), half * EH:(half + 1) * EH]
                                      .rearrange("p t e -> p (t e)").unsqueeze(2).to_broadcast([P, EH, D]),
                                      ALU.mult).then_inc(eo_out, 1)

            for j in range(HJ):
                dve.wait_ge(hid_top, it * HJ + j + 1)
                hi, lo = (t[j % 4][:, :, :].rearrange("p i n -> p (i n)") for t in (hid_hi, hid_lo))
                dve.scalar_tensor_tensor(lo, bank[j % 4][:, :], 0.0, hi, ALU.max, ALU.subtract).then_inc(hid_out, 1)
                if j == 5:
                    gated(0)
            gated(1)
        turn(0)
        with dve.Fori(1, NI) as it:
            turn(it)

        dve.wait_ge(moe_sum, NT)
        fdone = [0]

        def fstep(ins):
            fdone[0] += 1
            ins.then_inc(fin_step, 1)
            dve.wait_ge(fin_step, fdone[0])

        fstep(dve.tensor_tensor(xn[:, :, :], xn[:, :, :], sq[:, :, :], ALU.add))
        layer_norm(dve, 2, xn)
        big = [P, NT, D]
        fstep(dve.tensor_tensor(xn[:, :, :], xn[:, :, :], ln[:, 7, :].unsqueeze(2).to_broadcast(big), ALU.mult))
        fstep(dve.tensor_tensor(xn[:, :, :], xn[:, :, :], gamma[:, :].unsqueeze(1).to_broadcast(big), ALU.mult))
        fstep(dve.tensor_tensor(xn[:, :, :], xn[:, :, :], beta[:, :].unsqueeze(1).to_broadcast(big), ALU.add))
        fstep(dve.tensor_tensor(h[:, :, :], h[:, :, :], xn[:, :, :], ALU.add))
        assert fdone[0] == FIN_STEPS + 1

    return sync, gpsimd, tensor, scalar, vector


def transforms():
    y = np.arange(S)
    ky = np.arange(M2)
    kx = np.concatenate([np.arange(M1), np.arange(S - M1, S)])
    ay = 2 * np.pi * np.outer(y, ky) / S
    ax = 2 * np.pi * np.outer(y, kx) / S
    col = np.stack([np.cos(ay), -np.sin(ay)], -1)
    fwd_y = np.zeros((2, S, 2, M2, 2))
    for h in range(2):
        fwd_y[h, :, h] = col
    fwd_x = np.zeros((S, 2, KX, 2))
    fwd_x[:, 0, :, 0], fwd_x[:, 0, :, 1] = np.cos(ax), -np.sin(ax)
    fwd_x[:, 1, :, 0], fwd_x[:, 1, :, 1] = np.sin(ax), np.cos(ax)
    inv_x = np.zeros((KX, 2, S, 2))
    inv_x[:, 0, :, 0], inv_x[:, 0, :, 1] = np.cos(ax).T, np.sin(ax).T
    inv_x[:, 1, :, 0], inv_x[:, 1, :, 1] = -np.sin(ax).T, np.cos(ax).T
    weight = np.where(ky == 0, 1.0, 2.0) / (PX // 64)
    back = np.stack([np.cos(ay) * weight, -np.sin(ay) * weight], 1)
    inv_y = np.zeros((2, 2, M2, 2, 2, S))
    for q in range(2):
        inv_y[q, :, :, :, q, :] = back.transpose(2, 1, 0)
    line = np.linspace(0.0, 1.0, S, dtype=np.float32)
    grid = np.stack([np.repeat(line, S), np.tile(line, S), np.ones(PX, np.float32)])
    full = np.fft.fft2(grid.reshape(3, S, S).astype(np.float64))[:, kx][:, :, ky]
    parts = np.stack([full.real, full.imag], -1).reshape(3, KX, KYH, KY4, 2)
    gspec = parts.transpose(0, 3, 2, 1, 4).reshape(3 * KY4, SPEC)
    f = lambda a, *shape: np.ascontiguousarray(a.reshape(shape), np.float32)

    def split(a, rows, cols):
        a = a.reshape(rows, cols)
        hi = a.astype(np.float16)
        return np.stack([hi, (a - hi).astype(np.float16)], 1)
    return dict(fwd_y=split(fwd_y / 8, P, 48), fwd_x=split(fwd_x / 8, P, 48), inv_x=np.tile(split(inv_x, 48, P), (2, 1, 1)), inv_y=split(inv_y, 96, P),
                grid=grid, gspec=f(np.tile(gspec / 64, (1, F0B)), 12, FQ))


def kernel(**inputs):
    import concourse.bacc as bacc
    from concourse.bass_utils import run_bass_kernel_spmd

    a = {n.replace("L0_", ""): np.asarray(t) for n, t in inputs.items()}
    eye = np.eye(P, dtype=np.float32)
    same = np.kron(np.ones((GI, GI), np.float32), np.eye(C, dtype=np.float32))
    arrays = dict(transforms(), x=a["x"].reshape(NG, GI, PX), ident=eye, ident16=eye.astype(np.float16), avg=same / GI,
                  quarter=np.full((P, P), 1 / GI, np.float32))

    fw = np.concatenate([a["tok_fw1"], a["tok_fw2"]], axis=3)
    fw = fw.reshape(L, C, C, KX, KYH, KY4, 2).transpose(0, 4, 3, 5, 1, 6, 2)
    fw = fw.reshape(L * NCH, CH, P, 2 * C).transpose(0, 2, 1, 3)
    arrays["fw"] = np.ascontiguousarray(fw).reshape(L * NCH, P, CH * 2 * C)
    wmix = np.zeros((GI, C, L, GI, C), np.float32)
    p16 = np.zeros((4, KY4, KY4, C), np.float32)
    pt7 = np.zeros((GI, C, 96), np.float32)
    qbd = np.zeros((GI, C, GI + 1), np.float32)
    lift = [a["tok_p_w"][0], a["tok_p_w"][1], a["tok_p_w"][2], a["tok_p_b"]]
    for j in range(GI):
        wmix[j, :, :, j, :] = a["tok_w_w"].transpose(1, 0, 2)
        for at in X7_ROWS:
            pt7[j, :, at + j] = lift[0]
        for f in range(4):
            p16[f, j, j] = lift[f]
        for f in range(3):
            for at in X7_ROWS:
                pt7[j, :, at + GI + f] = lift[1 + f]
        qbd[j, :, j] = a["tok_q_w"][:, 0]
        qbd[j, :, GI] = a["tok_q_w"][:, 0]
    chan = np.stack([a["tok_w_b"].T, a["tok_bn_g"].T, a["tok_bn_b"].T], -1)
    arrays.update(wmix=wmix.reshape(P, L, P), p16=p16.reshape(16, P), pt7=pt7.reshape(P, 96), qbd=qbd.reshape(P, GI + 1),
                  chan=np.tile(chan, (GI, 1, 1)), qb=np.tile(a["tok_q_b"].reshape(1, 1), (P, 1)))

    w_qkv = a["attn_w_qkv"].reshape(3, S, S)
    wqk = np.stack([np.stack([w_qkv[i].T] * 2, 1) for i in range(2)], 1)
    tokens = np.arange(P)
    heads = np.repeat(np.arange(H), HD)
    parity = (tokens[:, None] // S == np.tile(heads, 2)[None, :] % 2)
    arrays.update(
        att_ident=eye, att_ident16=eye.astype(np.float16), att_wqk=wqk.reshape(S, 4 * S), att_wv=w_qkv[2].T,
        att_wp=np.concatenate([a["attn_w_proj"].T, a["attn_b_proj"][None, :]]),
        att_head_mask=(np.tile(heads, 2)[:, None] == np.arange(H)).astype(np.float32), att_v_mask=parity.astype(np.float32),
        att_iota=np.stack([tokens, tokens + P], 1).astype(np.float32), att_table=a["attn_rel_table"],
        att_index=a["attn_rel_index"].reshape(1, NIDX))
    b1 = np.zeros((33, NE * FF), np.float32)
    b1[[0, 32]] = a["ffn_b1"].reshape(NE * FF)
    b2 = np.zeros((8, NE, 8, D), np.float32)
    for i in range(8):
        b2[i, :, i, :] = a["ffn_b2"]
    arrays.update(
        moe_gw=np.tile(a["ffn_gate_w"], (2, 1)), moe_gb=np.tile(a["ffn_gate_b"][None, :], (P, 1)),
        moe_w1=np.tile(a["ffn_w1"].transpose(1, 0, 2).reshape(D, NE * FF), (2, 1)), moe_b1=b1,
        moe_w2=a["ffn_w2"].transpose(1, 0, 2).reshape(FF, NE * D), moe_b2=b2.reshape(P, 8 * D),
        moe_gamma=np.tile(a["ffn_gamma"][None, :], (P, 1)), moe_beta=np.tile(a["ffn_beta"][None, :], (P, 1)),
        moe_erow=np.tile(np.arange(NE, dtype=np.float32)[None, :], (P, 1)))

    nc = bacc.Bacc("TRN2", target_bir_lowering=False, num_devices=1)
    arrays = {n: np.ascontiguousarray(t) for n, t in arrays.items()}
    d = {n: nc.dram_tensor(n, t.shape, mybir.dt.from_np(t.dtype), kind="ExternalInput").ap() for n, t in arrays.items()}
    att = {n[4:]: d.pop(n) for n in list(d) if n.startswith("att_")}
    moe = {n[4:]: d.pop(n) for n in list(d) if n.startswith("moe_")}
    out = nc.dram_tensor("out", (B, S, S), F32, kind="ExternalOutput").ap()
    build(nc, out=out, att=att, moe=moe, **d)
    r = run_bass_kernel_spmd(nc, [arrays], core_ids=[0])
    return r.results[0]["out"]
```
